# Optimizing a Trainium2 kernel written in Bass

```python
import numpy as np
import jax
import jax.numpy as jnp

def _softmax(x, axis=-1):
    return jax.nn.softmax(x, axis=axis)

def _gelu(x):
    return jax.nn.gelu(x, approximate=True)

def _silu(x):
    return jax.nn.silu(x)

def _sigmoid(x):
    return jax.nn.sigmoid(x)

def _layernorm(x, axis=-1, eps=1e-05):
    m = jnp.mean(x, axis=axis, keepdims=True)
    v = jnp.var(x, axis=axis, keepdims=True)
    return (x - m) / jnp.sqrt(v + eps)

def _scatter_add(tgt, idx, src, axis=0):
    return tgt.at[idx].add(src)

def _segment_sum(src, seg, n):
    return jax.ops.segment_sum(src, seg, n)
kernel_name = 'mk_adaln_d1_jaxref_r2_6effe8'

def setup_inputs(seed: int=0):
    np.random.seed(seed)
    _w = jnp.asarray

    def _L0_attn_setup():
        import jax, jax.numpy as jnp
        import numpy as np
        B, T, C, H = (2, 1024, 512, 16)
        HS = C // H

        def _rope_cos_sin(t, hs):
            pos = jnp.arange(t, dtype=jnp.float32)[:, None]
            i = jnp.arange(1, hs // 2 + 1, dtype=jnp.float32)[None]
            theta = 1.0 / 10000.0 ** (2.0 * (i - 1.0) / hs)
            ang = pos * theta
            return (jnp.cos(ang), jnp.sin(ang))

        def _apply_rope(u, cos, sin):
            u2 = u.reshape(*u.shape[:-1], HS // 2, 2)
            x0, x1 = (u2[..., 0], u2[..., 1])
            c = cos[None, None]
            s = sin[None, None]
            r0 = x0 * c - x1 * s
            r1 = x0 * s + x1 * c
            return jnp.stack([r0, r1], axis=-1).reshape(u.shape)
        key = jax.random.key(seed)
        ks = jax.random.split(key, 5)
        return {'x': jax.random.normal(ks[0], (B, T, C), dtype=jnp.float32), 'W_qkv': jax.random.normal(ks[1], (C, 3 * C), dtype=jnp.float32) * 0.02, 'b_qkv': jax.random.normal(ks[2], (3 * C,), dtype=jnp.float32) * 0.02, 'W_proj': jax.random.normal(ks[3], (C, C), dtype=jnp.float32) * 0.02, 'b_proj': jax.random.normal(ks[4], (C,), dtype=jnp.float32) * 0.02}
    _L0_attn_in = _L0_attn_setup()

    def _L0_ffn_setup():
        import jax, jax.numpy as jnp
        import numpy as np
        S, B, D, H, DH = (2048, 8, 512, 16, 64)

        def _forward(x, Wg, Wq, bq, Wkv, bkv, Wo, bo, ln_g, ln_b):
            s_len, bsz, d_model = x.shape
            n_head, _, d_head = Wq.shape
            cap = s_len // n_head
            scale = 1.0 / d_head ** 0.5
            h = jnp.transpose(x, (1, 0, 2))
            t = h
            probs = jax.nn.softmax(h @ Wg, axis=-1)
            scores = jnp.transpose(probs, (0, 2, 1))
            _, idx = jax.lax.top_k(scores, cap)
            idx = jnp.sort(idx, axis=-1)
            hg = jnp.take_along_axis(h[:, None, :, :], idx[..., None], axis=2)
            hg = jnp.transpose(hg, (1, 0, 2, 3))
            q = jnp.einsum('hbcd,hde->hbce', hg, Wq) + bq[:, None, None, :]
            kv = jnp.einsum('hbcd,hde->hbce', hg, Wkv) + bkv[:, None, None, :]
            k, v = jnp.split(kv, 2, axis=-1)
            att = jnp.einsum('hbid,hbjd->hbij', q, k) * scale
            p = jax.nn.softmax(att, axis=1)
            av = jnp.einsum('hbij,hbjd->hbid', p, v)
            ao = jnp.einsum('hbid,hde->hbie', av, Wo) + bo
            tok = jnp.transpose(idx, (1, 0, 2))
            b_ids = jnp.arange(bsz)[None, :, None]
            outs = jnp.zeros_like(t).at[b_ids, tok].add(ao)
            y = t + outs
            mu = jnp.mean(y, axis=-1, keepdims=True)
            var = jnp.var(y, axis=-1, keepdims=True)
            yn = (y - mu) * jax.lax.rsqrt(var + 1e-05) * ln_g + ln_b
            return jnp.transpose(yn, (1, 0, 2))
        key = jax.random.key(seed)
        ks = jax.random.split(key, 6)
        s = 0.02
        return {'x': jax.random.normal(ks[0], (S, B, D), jnp.float32), 'attn_mask': jnp.zeros((S, S), jnp.bool_), 'Wg': jax.random.normal(ks[1], (D, H), jnp.float32) * s, 'Wq': jax.random.normal(ks[2], (H, D, DH), jnp.float32) * s, 'bq': jnp.zeros((H, DH), jnp.float32), 'Wkv': jax.random.normal(ks[3], (H, D, 2 * DH), jnp.float32) * s, 'bkv': jnp.zeros((H, 2 * DH), jnp.float32), 'Wo': jax.random.normal(ks[4], (H, DH, D), jnp.float32) * s, 'bo': jnp.zeros((D,), jnp.float32), 'ln_g': jnp.ones((D,), jnp.float32), 'ln_b': jnp.zeros((D,), jnp.float32)}
    _L0_ffn_in = _L0_ffn_setup()
    _L0_c = _w((lambda *s: np.random.randn(*s).astype(np.float32) * 0.05)(4, 512))
    _L0_wmod = _w((lambda *s: np.random.randn(*s).astype(np.float32) * 0.05)(512, 6 * 512) * 512 ** (-0.5))
    _d = {'L0_attn_x': _L0_attn_in['x'], 'L0_attn_W_qkv': _L0_attn_in['W_qkv'], 'L0_attn_b_qkv': _L0_attn_in['b_qkv'], 'L0_attn_W_proj': _L0_attn_in['W_proj'], 'L0_attn_b_proj': _L0_attn_in['b_proj'], 'L0_ffn_attn_mask': _L0_ffn_in['attn_mask'], 'L0_ffn_Wg': _L0_ffn_in['Wg'], 'L0_ffn_Wq': _L0_ffn_in['Wq'], 'L0_ffn_bq': _L0_ffn_in['bq'], 'L0_ffn_Wkv': _L0_ffn_in['Wkv'], 'L0_ffn_bkv': _L0_ffn_in['bkv'], 'L0_ffn_Wo': _L0_ffn_in['Wo'], 'L0_ffn_bo': _L0_ffn_in['bo'], 'L0_ffn_ln_g': _L0_ffn_in['ln_g'], 'L0_ffn_ln_b': _L0_ffn_in['ln_b'], 'L0_c': _L0_c, 'L0_wmod': _L0_wmod}
    _x0 = _d['L0_attn_x']
    _d['L0_attn_x'] = jax.random.normal(jax.random.fold_in(jax.random.key(seed), 1), (4, 2048, 512), dtype=_x0.dtype)
    del _x0
    return _d

def reference(L0_attn_x, L0_attn_W_qkv, L0_attn_b_qkv, L0_attn_W_proj, L0_attn_b_proj, L0_ffn_attn_mask, L0_ffn_Wg, L0_ffn_Wq, L0_ffn_bq, L0_ffn_Wkv, L0_ffn_bkv, L0_ffn_Wo, L0_ffn_bo, L0_ffn_ln_g, L0_ffn_ln_b, L0_c, L0_wmod):

    def _L0_attn_ref(x, W_qkv, b_qkv, W_proj, b_proj):
        import jax, jax.numpy as jnp
        import numpy as np
        B, T, C, H = (2, 1024, 512, 16)
        HS = C // H

        def _rope_cos_sin(t, hs):
            pos = jnp.arange(t, dtype=jnp.float32)[:, None]
            i = jnp.arange(1, hs // 2 + 1, dtype=jnp.float32)[None]
            theta = 1.0 / 10000.0 ** (2.0 * (i - 1.0) / hs)
            ang = pos * theta
            return (jnp.cos(ang), jnp.sin(ang))

        def _apply_rope(u, cos, sin):
            u2 = u.reshape(*u.shape[:-1], HS // 2, 2)
            x0, x1 = (u2[..., 0], u2[..., 1])
            c = cos[None, None]
            s = sin[None, None]
            r0 = x0 * c - x1 * s
            r1 = x0 * s + x1 * c
            return jnp.stack([r0, r1], axis=-1).reshape(u.shape)
        b, t, c = x.shape
        qkv = x @ W_qkv + b_qkv
        qkv = qkv.reshape(b, t, H, 3 * HS).transpose(0, 2, 1, 3)
        q, k, v = jnp.split(qkv, 3, axis=-1)
        cos, sin = _rope_cos_sin(t, HS)
        q = _apply_rope(q, cos, sin)
        k = _apply_rope(k, cos, sin)
        att = jnp.einsum('bhqd,bhkd->bhqk', q, k) / jnp.sqrt(jnp.float32(HS))
        causal = jnp.tril(jnp.ones((t, t), dtype=bool))[None, None]
        att = jnp.where(causal, att, jnp.float32(-1000000000.0))
        att = jax.nn.softmax(att, axis=-1)
        y = jnp.einsum('bhqk,bhkd->bhqd', att, v)
        y = y.transpose(0, 2, 1, 3).reshape(b, t, c)
        return y @ W_proj + b_proj

    def _L0_ffn_ref(x, attn_mask, Wg, Wq, bq, Wkv, bkv, Wo, bo, ln_g, ln_b):
        import jax, jax.numpy as jnp
        import numpy as np
        S, B, D, H, DH = (2048, 8, 512, 16, 64)

        def _forward(x, Wg, Wq, bq, Wkv, bkv, Wo, bo, ln_g, ln_b):
            s_len, bsz, d_model = x.shape
            n_head, _, d_head = Wq.shape
            cap = s_len // n_head
            scale = 1.0 / d_head ** 0.5
            h = jnp.transpose(x, (1, 0, 2))
            t = h
            probs = jax.nn.softmax(h @ Wg, axis=-1)
            scores = jnp.transpose(probs, (0, 2, 1))
            _, idx = jax.lax.top_k(scores, cap)
            idx = jnp.sort(idx, axis=-1)
            hg = jnp.take_along_axis(h[:, None, :, :], idx[..., None], axis=2)
            hg = jnp.transpose(hg, (1, 0, 2, 3))
            q = jnp.einsum('hbcd,hde->hbce', hg, Wq) + bq[:, None, None, :]
            kv = jnp.einsum('hbcd,hde->hbce', hg, Wkv) + bkv[:, None, None, :]
            k, v = jnp.split(kv, 2, axis=-1)
            att = jnp.einsum('hbid,hbjd->hbij', q, k) * scale
            p = jax.nn.softmax(att, axis=1)
            av = jnp.einsum('hbij,hbjd->hbid', p, v)
            ao = jnp.einsum('hbid,hde->hbie', av, Wo) + bo
            tok = jnp.transpose(idx, (1, 0, 2))
            b_ids = jnp.arange(bsz)[None, :, None]
            outs = jnp.zeros_like(t).at[b_ids, tok].add(ao)
            y = t + outs
            mu = jnp.mean(y, axis=-1, keepdims=True)
            var = jnp.var(y, axis=-1, keepdims=True)
            yn = (y - mu) * jax.lax.rsqrt(var + 1e-05) * ln_g + ln_b
            return jnp.transpose(yn, (1, 0, 2))
        return _forward(x, Wg, Wq, bq, Wkv, bkv, Wo, bo, ln_g, ln_b)
    x = L0_attn_x
    mod = (_silu(L0_c) @ L0_wmod).reshape(L0_c.shape[0], 6, 1, -1)
    sa, ca, ga, sb, cb, gb = (mod[:, 0], mod[:, 1], mod[:, 2], mod[:, 3], mod[:, 4], mod[:, 5])
    ga = (2 * (ga >= 0) - 1) * jnp.maximum(jnp.abs(ga), 0.25)
    gb = (2 * (gb >= 0) - 1) * jnp.maximum(jnp.abs(gb), 0.25)
    h = _layernorm(x, axis=-1) * (1 + ca) + sa
    x = x + ga * _L0_attn_ref(h, L0_attn_W_qkv, L0_attn_b_qkv, L0_attn_W_proj, L0_attn_b_proj)
    h = _layernorm(x, axis=-1) * (1 + cb) + sb
    x = x + gb * _L0_ffn_ref(h, L0_ffn_attn_mask, L0_ffn_Wg, L0_ffn_Wq, L0_ffn_bq, L0_ffn_Wkv, L0_ffn_bkv, L0_ffn_Wo, L0_ffn_bo, L0_ffn_ln_g, L0_ffn_ln_b)
    return x

_drawn_inputs = setup_inputs


def setup_inputs(seed=0):
    import zlib

    import numpy as np

    out = dict(_drawn_inputs(seed))
    spreads = {'L0_ffn_bq': (0.0, 0.1),
     'L0_ffn_bkv': (0.0, 0.1),
     'L0_ffn_bo': (0.0, 0.1),
     'L0_ffn_ln_g': (1.0, 0.6),
     'L0_ffn_ln_b': (0.0, 0.996)}
    factors = {'L0_attn_W_qkv': 8.0,
     'L0_attn_b_qkv': 8.0,
     'L0_attn_W_proj': 8.0,
     'L0_attn_b_proj': 35.051}
    for name, (base, spread) in spreads.items():
        noise = np.random.default_rng([zlib.crc32(name.encode()), seed]).standard_normal(out[name].shape)
        drawn = base * np.exp(spread * noise) if base else spread * noise
        out[name] = jnp.asarray(drawn.astype(out[name].dtype))
    for name, factor in factors.items():
        out[name] = (out[name] * factor).astype(out[name].dtype)
    return out
```

```python
from contextlib import ExitStack

import concourse.bass as bass
from concourse import mybir

ALU = mybir.AluOpType
ACT = mybir.ActivationFunctionType
AX = mybir.AxisListType
F32 = mybir.dt.float32
F16 = mybir.dt.float16
BF16 = mybir.dt.bfloat16

P = 128
EPS = 1e-5
W_SCALE = 64.0
M_SCALE = 256.0
MASKED = -1e30


def wait_value(count):
    return max(count, 0) if isinstance(count, int) else count


def adaln_block_kernel(nc, x, w_qkv, b_qkv, w_proj, b_proj, ln_g, ln_b, c, w_mod, rope_cos, rope_sin, out):
    B, T, C = x.shape
    N_QKV = w_qkv.shape[1]
    HS = 32
    H = C // HS
    HG = P // HS
    NG = H // HG
    KC = C // P
    NT = T // P
    QC = 512
    TPC = QC // P
    NC_ = T // QC
    GW = HG * 3 * HS
    R = 3 * HS
    RM = R + 2
    SCALE = float(HS) ** -0.5
    STEPS = [(cq, kt) for cq in range(NC_) for kt in range(TPC * (cq + 1))]
    UNITS = [(qt, kc) for qt in range(NT) for kc in range(qt // TPC + 1)]
    NS = len(STEPS)
    assert len(UNITS) == NS

    TAIL_STEPS = {0: {2 + 5 * k: k for k in range(NT // 2)}, 1: {2 + 5 * k: NT // 2 + k for k in range(NT // 2)}}
    HEAD_STEPS = {2: {6 + 2 * k: k for k in range(NT)}}
    RING = NG * NS * HG + 2 * NT

    ot_d = nc.dram_tensor("attn_out_T", (B, P, NG, 2, T), F16, kind="Internal").ap()
    mod_d = nc.dram_tensor("modulation", (B, 8, C), F32, kind="Internal").ap()

    with ExitStack() as ctx:
        def sb(name, shape, dt):
            return ctx.enter_context(nc.sbuf_tensor(name, shape, dt))

        def sem(name):
            return ctx.enter_context(nc.semaphore(name))

        hT = sb("hT", [P, 2, KC, T], F16)
        w16 = sb("w16", [P, 2, KC, N_QKV], F16)
        wp16 = sb("wp16", [P, 2, KC, C], F16)
        qk = sb("qk", [P, 2, 2, HG, T], F16)
        v32 = sb("v32", [P, 2, NT, HG * HS], F32)
        prob = sb("prob", [P, 2, 2, 2, QC], F32)
        bc = sb("bc", [P, 6, C], F32)
        bqkv = sb("bqkv", [P, N_QKV], F32)
        cos_sb = sb("cos_sb", [P, NT, HS], F32)
        sin_sb = sb("sin_sb", [P, NT, HS], F32)
        xs = sb("xs", [P, 2, C], F32)
        wk = sb("wk", [P, 2, C], F32)
        x1 = sb("x1", [P, 2, C], F32)
        otin = sb("otin", [P, 2, NG, 2, 2 * P], F16)
        qk32 = sb("qk32", [P, 3, 2 * HG, HS], F32)
        ropeA = sb("ropeA", [P, 2, 2 * HG, HS], F32)
        ropeB = sb("ropeB", [P, 2 * HG, HS], F32)
        ropeR = qk32[:].rearrange("p s (h two) n -> p s h two n", two=2)
        qk16 = sb("qk16", [P, 3, HG, 2 * R], F16)
        onrm = sb("onrm", [P, QC], F32)
        ot16 = sb("ot16", [P, 2, 2, QC], F16)
        mpart = sb("mpart", [P, HG, NT, NC_], F32)
        nmax = sb("nmax", [P, HG * NT], F32)
        nm16 = sb("nm16", [P, 2, HG * NT], F16)
        mrow = sb("mrow", [P, P], F16)
        ident = sb("ident", [P, P], F32)
        ident16 = sb("ident16", [P, P], F16)
        identb = sb("identb", [P, P], BF16)
        mask_qk = sb("mask_qk", [P, P], BF16)
        mask_kq = sb("mask_kq", [P, P], BF16)
        ones = sb("ones", [P, HS], F32)
        cT = sb("cT", [P, KC, B], F32)
        eT = sb("eT", [P, KC, B], F32)
        colmod = sb("colmod", [P, 2, KC], F32)
        stats = sb("stats", [P, 2, 6], F32)
        mv = sb("mv", [P, 2, 2], F32)
        mv2 = sb("mv2", [P, 2, 2], F32)
        rstd = sb("rstd", [P, 2, 1], F32)
        rstd2 = sb("rstd2", [P, 2, 1], F32)
        vare = sb("vare", [P, 2, 1], F32)
        neg_half = sb("neg_half", [P, 1], F32)
        eps_t = sb("eps_t", [P, 1], F32)

        stage_w = hT[:].rearrange("p a k t -> p (a k t)").bitcast(F32)
        stage_wqkv = stage_w[:, 0:KC * N_QKV].rearrange("p (k n) -> p k n", k=KC)
        stage_wproj = stage_w[:, KC * N_QKV:KC * (N_QKV + C)].rearrange("p (k n) -> p k n", k=KC)
        stage_wmod = qk[:].rearrange("p a b h t -> p (a b h t)").bitcast(F32)[:, 0:KC * 6 * C].rearrange(
            "p (k n) -> p k n", k=KC)
        rows = prob[:].rearrange("p a b h q -> p (a b h q)")[0:B, :].rearrange("p (m n) -> p m n", n=C)
        prow = v32[:].rearrange("p a t n -> p (a t n)")[0:B, 0:5 * C].rearrange("p (m n) -> p m n", n=C)

        ps_s = [ctx.enter_context(nc.psum_tensor(f"ps_s{i}", [P, 2, QC], F32)) for i in range(2)]
        ps_o = ctx.enter_context(nc.psum_tensor("ps_o", [P, QC], F32))
        ps_d = ctx.enter_context(nc.psum_tensor("ps_d", [P, QC], F32))
        ring = [ctx.enter_context(nc.psum_tensor(f"ring{i}", [P, QC], F32)) for i in range(2)]
        ps_tr = [ps_s[1][:, i, :].bitcast(F16) for i in range(2)]

        c_ld, w_ld, wm_ld, row_ld, misc_ld = (sem(n) for n in ("c_ld", "w_ld", "wm_ld", "row_ld", "misc_ld"))
        consts, wsplit, silu_e, silu_done, mod_mm, mod_row = (
            sem(n) for n in ("consts", "wsplit", "silu_e", "silu_done", "mod_mm", "mod_row"))
        mod_read = sem("mod_read")
        mod_st, col_ld, bc_ld, one_rows = (sem(n) for n in ("mod_st", "col_ld", "bc_ld", "one_rows"))
        x_ld, ot_dma, ot_ld, out_dma = ([sem(f"{n}{i}") for i in range(2)] for n in ("x_ld", "ot_dma", "ot_ld", "out_dma"))
        head_stat, head_rstd, head_norm, head_done = (
            sem(n) for n in ("head_stat", "head_rstd", "head_norm", "head_done"))
        qkv_mm, qkv_evac, rope_a, rope_r, hi2, split, qk_tr, tr_evac = (
            sem(n) for n in ("qkv_mm", "qkv_evac", "rope_a", "rope_r", "hi2", "split", "qk_tr", "tr_evac"))
        ring_full, ring_free = sem("ring_full"), sem("ring_free")
        m_split, m_tr, m_cp, m_dma = (sem(n) for n in ("m_split", "m_tr", "m_cp", "m_dma"))
        st_mm, exp_done, pv_done, o_free, ot_split = (
            sem(n) for n in ("st_mm", "exp_done", "pv_done", "o_free", "ot_split"))
        tail_xg, tail_a, tail_r1, tail_xb, tail_c, tail_r2, tail_e = (
            sem(n) for n in ("tail_xg", "tail_a", "tail_r1", "tail_xb", "tail_c", "tail_r2", "tail_e"))

        def job_base(b):
            return NT // 2 if isinstance(b, int) and b == 0 else NT * b

        def ring_base(b):
            prologue = NT + NS * HG
            return prologue if isinstance(b, int) and b == 0 else prologue + RING * b - NT

        def batches(eng, body):
            body(0, first=True, last=False)
            with eng.Fori(1, B - 1) as b:
                body(b, first=False, last=False)
            body(B - 1, first=False, last=True)

        block = ctx.enter_context(nc.Block())

        @block.sync
        def _(sp):
            def load_x(b, t):
                sp.wait_ge(mod_st, 16)
                sp.dma_start(xs[:, t % 2, :], x[b, t * P:(t + 1) * P, :]).then_inc(x_ld[t % 2], 16)

            def load_columns(b):
                with nc.allow_non_contiguous_dma(reason="a batch's columns of the modulation, 1024 words"):
                    for i in range(2):
                        sp.dma_start(colmod[:, i, :], mod_d[b, i, :].rearrange("(k p) -> p k", p=P)).then_inc(col_ld, 16)

            sp.dma_start(stage_wqkv, w_qkv.rearrange("(k p) n -> p k n", p=P)).then_inc(w_ld, 16)
            sp.dma_start(stage_wproj, w_proj.rearrange("(k p) n -> p k n", p=P)).then_inc(w_ld, 16)
            with nc.allow_non_contiguous_dma(reason="c transposed, 2048 words"):
                for k in range(KC):
                    sp.dma_start(cT[:, k, :], c[:, k * P:(k + 1) * P].rearrange("b p -> p b")).then_inc(c_ld, 16)
            sp.dma_start(stage_wmod, w_mod.rearrange("(k p) n -> p k n", p=P)).then_inc(wm_ld, 16)
            for i, row in enumerate((b_proj, ln_g, ln_b)):
                sp.dma_start(prow[:, i, :], row.rearrange("(a n) -> a n", a=1).to_broadcast([B, C])).then_inc(row_ld, 16)
            sp.dma_start(bqkv[:], b_qkv.rearrange("(a n) -> a n", a=1).to_broadcast([P, N_QKV])).then_inc(misc_ld, 16)
            sp.dma_start(cos_sb[:], rope_cos.rearrange("(t p) n -> p t n", p=P)).then_inc(misc_ld, 16)
            sp.dma_start(sin_sb[:], rope_sin.rearrange("(t p) n -> p t n", p=P)).then_inc(misc_ld, 16)
            sp.wait_ge(mod_row, 1)
            sp.dma_start(mod_d, rows).then_inc(mod_st, 16)
            sp.wait_ge(mod_st, 16)
            load_columns(0)
            for t in range(NT):
                if t >= 2:
                    sp.wait_ge(head_norm, t - 1)
                load_x(0, t)

            def maxima_rows(G, par):
                sp.wait_ge(m_cp, G + 1)
                for i in range(2):
                    sp.dma_start(qk[R + i:R + i + 1, par, 0, :, :].rearrange("p h (t q) -> p (h t) q", q=P),
                                 mrow[i * HG * NT:(i + 1) * HG * NT, :]).then_inc(m_dma, 16)

            def tail_loads(b, t, heads):
                Z = NT * b + t
                if t == 0:
                    sp.wait_ge(tail_e, wait_value(Z))
                    sp.wait_ge(mod_st, 16)
                    sp.dma_start(bc[:], mod_d[b, 2:8, :].rearrange("(a m) n -> a m n", a=1).to_broadcast(
                        [P, 6, C])).then_inc(bc_ld, 16)
                    for i in range(2):
                        sp.wait_ge(ot_dma[i], 16 * NG * NC_ // 2 * (b + 1))
                    sp.wait_ge(head_norm, heads)
                if t % 2 == 0:
                    if t >= 4:
                        sp.wait_ge(tail_a, Z - 2)
                    sp.wait_ge(mod_st, 16)
                    sp.dma_start(otin[:, t // 2 % 2], ot_d[b, :, :, :, t * P:(t + 2) * P]).then_inc(ot_ld[t // 2 % 2], 16)
                if t >= 2:
                    sp.wait_ge(tail_e, Z - 1)
                load_x(b, t)

            def store_out(b, t):
                sp.wait_ge(tail_e, NT * b + t + 1)
                sp.wait_ge(mod_st, 16)
                sp.dma_start(out[b, t * P:(t + 1) * P, :], x1[:, t % 2, :]).then_inc(out_dma[t % 2], 16)

            def body(b, first, last):
                for g in range(NG):
                    maxima_rows(NG * b + g, g % 2)
                    for s, (cq, kt) in enumerate(STEPS):
                        if not first and g in TAIL_STEPS:
                            at = TAIL_STEPS[g]
                            if s + 2 in at:
                                tail_loads(b - 1, at[s + 2], NT * (b + 1))
                            if s - 2 in at:
                                store_out(b - 1, at[s - 2])
                        if not last and g in HEAD_STEPS:
                            at = HEAD_STEPS[g]
                            if s == 0:
                                load_columns(b + 1)
                            if s + 5 in at:
                                t = at[s + 5]
                                if t >= 2 or first:
                                    sp.wait_ge(head_norm, NT * (b + 1) + t - 1)
                                elif t == 0:
                                    sp.wait_ge(tail_e, NT * b)
                                load_x(b + 1, t)
                        if s > 0 and STEPS[s - 1][0] != cq:
                            store_ot(b, g, cq - 1)
                    store_ot(b, g, NC_ - 1)

            def store_ot(b, g, cq):
                sp.wait_ge(ot_split, NC_ * (NG * b + g) + cq + 1)
                sp.wait_ge(mod_st, 16)
                sp.dma_start(ot_d[b, :, g, :, cq * QC:(cq + 1) * QC], ot16[:, cq % 2]).then_inc(ot_dma[cq % 2], 16)

            batches(sp, body)
            for t in range(NT):
                if t >= 2:
                    store_out(B - 1, t - 2)
                tail_loads(B - 1, t, NT * B)
            for t in (NT - 2, NT - 1):
                store_out(B - 1, t)
            for i in range(2):
                sp.wait_ge(out_dma[i], 16 * B * NT // 2)

        @block.gpsimd
        def _(pool):
            pool.memset(ident[:], 0.0)
            pool.memset(ident16[:], 0.0)
            pool.memset(identb[:], 0.0)
            pool.memset(mask_qk[:], 0.0)
            pool.memset(mask_kq[:], 0.0)
            pool.memset(ones[:], 1.0)
            pool.memset(neg_half[:], -0.5)
            pool.memset(eps_t[:], EPS)
            pool.drain()
            for one in (ident, ident16, identb):
                pool.affine_select(out=one[:], in_=one[:], compare_op=ALU.not_equal, fill=1.0, base=0,
                                   pattern=[[-1, P]], channel_multiplier=1)
            pool.affine_select(out=mask_qk[:], in_=mask_qk[:], compare_op=ALU.is_ge, fill=MASKED, base=0,
                               pattern=[[-1, P]], channel_multiplier=1)
            pool.affine_select(out=mask_kq[:], in_=mask_kq[:], compare_op=ALU.is_ge, fill=MASKED, base=0,
                               pattern=[[1, P]], channel_multiplier=-1)
            pool.drain().then_inc(consts, 1)

            def inv_std(dst, src):
                pool.tensor_tensor(vare[:, 0, :], src[:, 1:2], eps_t[:], ALU.add)
                pool.drain()
                return pool.tensor_tensor(dst, vare[:, 0, :], neg_half[:], ALU.pow)

            def head_tile(b, t):
                pool.wait_ge(head_stat, NT * b + t + 1)
                inv_std(rstd[:, t % 2, :], mv[:, t % 2, :]).then_inc(head_rstd, 1)

            def rope_tile(G, t):
                N = NT * G + t
                pool.wait_ge(qkv_evac, N + 1)
                pool.wait_ge(rope_r, wait_value(N - 1))
                pool.tensor_tensor(ropeA[:, t % 2], qk32[:, t % 3],
                                   cos_sb[:, t:t + 1, :].to_broadcast([P, 2 * HG, HS]), ALU.mult).then_inc(rope_a, 1)

            def tail_x(b, t, job):
                if t == 0:
                    pool.wait_ge(bc_ld, 16 * (b + 1))
                pool.wait_ge(x_ld[t % 2], 16 * (job + 1))
                pool.tensor_tensor(xs[:, t % 2, :], xs[:, t % 2, :], bc[:, 1, :], ALU.add).then_inc(tail_xg, 1)

            def tail_1(b, t):
                pool.wait_ge(tail_a, NT * b + t + 1)
                inv_std(rstd[:, t % 2, :], mv[:, t % 2, :]).then_inc(tail_r1, 1)
                pool.tensor_tensor(xs[:, t % 2, :], x1[:, t % 2, :], bc[:, 5, :], ALU.add).then_inc(tail_xb, 1)

            def tail_2(b, t):
                pool.drain()
                pool.wait_ge(tail_c, NT * b + t + 1)
                inv_std(rstd2[:, t % 2, :], mv2[:, t % 2, :]).then_inc(tail_r2, 1)

            for t in range(NT):
                pool.drain()
                head_tile(0, t)
            pool.wait_ge(misc_ld, 48)
            for t in range(NT):
                rope_tile(0, t)

            def body(b, first, last):
                jobs = job_base(b)
                for g in range(NG):
                    if not (last and g == NG - 1):
                        for t in range(NT):
                            rope_tile(NG * b + g + 1, t)
                    pool.drain()
                    for s in range(NS):
                        if not first and g in TAIL_STEPS:
                            at = TAIL_STEPS[g]
                            if s in at:
                                tail_x(b - 1, at[s], jobs + at[s] // 2)
                                tail_1(b - 1, at[s])
                            if s - 1 in at:
                                tail_2(b - 1, at[s - 1])
                                pool.drain()
                        if not last and g in HEAD_STEPS and s + 2 in HEAD_STEPS[g]:
                            head_tile(b + 1, HEAD_STEPS[g][s + 2])
                            pool.drain()

            batches(pool, body)
            for t in range(NT):
                tail_x(B - 1, t, NT * (2 * B - 1) // 2 + t // 2)
                tail_1(B - 1, t)
                tail_2(B - 1, t)
                pool.drain()

        @block.scalar
        def _(act):
            act.wait_ge(c_ld, 16 * KC)
            act.activation(eT[:], cT[:], ACT.Exp, scale=-1.0).then_inc(silu_e, 1)

            def second_hi(G, t):
                N = NT * G + t
                act.wait_ge(rope_r, N + 1)
                act.wait_ge(qk_tr, wait_value(N - 2))
                act.copy(qk16[:, t % 3, :, HS:2 * HS], ropeR[:, t % 3, :, 0, :])
                act.copy(qk16[:, t % 3, :, R + 2 * HS:R + 3 * HS], ropeR[:, t % 3, :, 1, :]).then_inc(hi2, 1)

            def transposed(G, par, t):
                act.wait_ge(qk_tr, NT * G + t + 1)
                act.copy(qk[0:R, par, :, :, t * P:(t + 1) * P].rearrange("p two h q -> p (two h) q"),
                         ps_tr[t % 2][0:R, :].rearrange("p (n q) -> p n q", q=P)).then_inc(tr_evac, 1)

            def qkv(G, par):
                for t in range(NT + 3):
                    if t < NT:
                        second_hi(G, t)
                    if t >= 3:
                        transposed(G, par, t - 3)

            def maxima(G):
                act.wait_ge(m_tr, G + 1)
                act.wait_ge(m_dma, 32 * G)
                act.copy(mrow[:], ring[0][:, 0:P // 2].bitcast(F16)).then_inc(m_cp, 1)

            qkv(0, 0)

            def body(b, first, last):
                for g in range(NG):
                    G = NG * b + g
                    maxima(G)
                    if not (last and g == NG - 1):
                        qkv(G + 1, (g + 1) % 2)
                    for s, (cq, kt) in enumerate(STEPS):
                        w = QC - P * max(kt - TPC * cq, 0)
                        S = NS * G + s
                        for p in range(2):
                            act.wait_ge(st_mm, 2 * S + p + 1)
                            act.wait_ge(pv_done, wait_value(S - 1))
                            act.activation(prob[:, s % 2, p, :, 0:w], ps_s[p][:, :, 0:w], ACT.Exp,
                                           scale=SCALE).then_inc(exp_done, 1)

            batches(act, body)

        @block.vector
        def _(dve):
            dve.wait_ge(w_ld, 32)
            for st, dst in ((stage_wqkv, w16), (stage_wproj, wp16)):
                dve.tensor_scalar(st, st, W_SCALE, None, ALU.mult)
            dve.drain()
            for st, dst in ((stage_wqkv, w16), (stage_wproj, wp16)):
                dve.tensor_copy(dst[:, 0], st)
            dve.drain()
            dve.tensor_tensor(w16[:, 1], stage_wqkv, w16[:, 0], ALU.subtract)
            dve.tensor_tensor(wp16[:, 1], stage_wproj, wp16[:, 0], ALU.subtract).then_inc(wsplit, 1)
            dve.wait_ge(silu_e, 1)
            dve.tensor_scalar(eT[:], eT[:], 1.0, None, ALU.add)
            dve.drain()
            dve.reciprocal(eT[:], eT[:])
            dve.drain()
            dve.tensor_tensor(cT[:], cT[:], eT[:], ALU.mult).then_inc(silu_done, 1)
            dve.wait_ge(row_ld, 48)
            for j in range(6):
                dve.wait_ge(mod_mm, j + 1)
                src = ps_s[j % 2][0:B, 0, :]
                gate = prow[:, 3, :]
                sign = prow[:, 4, :]
                if j == 0:
                    dve.tensor_copy(rows[:, 0, :], src)
                elif j == 1:
                    dve.tensor_scalar(rows[:, 1, :], src, 1.0, None, ALU.add)
                elif j == 3:
                    dve.tensor_copy(rows[:, 5, :], src)
                elif j == 4:
                    dve.tensor_scalar(rows[:, 4, :], src, 1.0, None, ALU.add)
                else:
                    dve.tensor_copy(gate, src)
                    dve.drain()
                    dve.tensor_scalar(sign, gate, 0.0, 2.0, ALU.is_ge, ALU.mult)
                    dve.tensor_scalar(rows[:, 7, :], gate, -1.0, None, ALU.mult)
                    dve.drain()
                    dve.tensor_tensor(gate, gate, rows[:, 7, :], ALU.max)
                    dve.tensor_scalar(sign, sign, -1.0, None, ALU.add)
                    dve.drain()
                    dve.tensor_scalar(gate, gate, 0.25, None, ALU.max)
                    dve.drain()
                    dve.tensor_tensor(gate, gate, sign, ALU.mult)
                    dve.drain()
                    if j == 2:
                        dve.tensor_scalar(rows[:, 2, :], gate, 1.0 / W_SCALE, None, ALU.mult)
                        dve.tensor_tensor(rows[:, 3, :], gate, prow[:, 0, :], ALU.mult)
                    else:
                        dve.tensor_tensor(rows[:, 6, :], gate, prow[:, 1, :], ALU.mult)
                        dve.tensor_tensor(rows[:, 7, :], gate, prow[:, 2, :], ALU.mult)
                dve.drain().then_inc(mod_read, 1)
            dve.drain().then_inc(mod_row, 1)
            for par in range(2):
                dve.memset(qk[R:RM, par, 1, :, :], M_SCALE)
            dve.memset(mpart[:], -3e38)
            dve.drain().then_inc(one_rows, 1)

            def head_stats(b, t, job):
                dve.wait_ge(x_ld[t % 2], 16 * (job + 1))
                dve.wait_ge(head_rstd, wait_value(NT * b + t - 1))
                dve.bn_stats(stats[:, t % 2, :], xs[:, t % 2, :])
                dve.drain()
                dve.bn_aggr(mv[:, t % 2, :], stats[:, t % 2, :]).then_inc(head_stat, 1)

            def head_normed(b, t):
                dve.wait_ge(head_rstd, NT * b + t + 1)
                dve.tensor_scalar(wk[:, t % 2, :], xs[:, t % 2, :], mv[:, t % 2, 0:1], rstd[:, t % 2, :],
                                  ALU.subtract, ALU.mult).then_inc(head_norm, 1)

            def head_evac(b, t, use, n):
                if t == 0:
                    dve.wait_ge(col_ld, 32 * (b + 1))
                    for i in range(2):
                        dve.wait_ge(out_dma[i], wait_value(16 * NT // 2 * (b - 1)))
                dve.wait_ge(ring_full, use + 1)
                h32 = x1[:, t % 2, :].rearrange("p (k q) -> p k q", k=KC)
                src = ring[n % 2][:, :].rearrange("p (k q) -> p k q", k=KC)
                for k in range(KC):
                    normed = dve.tensor_scalar(h32[:, k, :], src[:, k, :], colmod[:, 1, k:k + 1], colmod[:, 0, k:k + 1],
                                               ALU.mult, ALU.add)
                normed.then_inc(ring_free, 1)
                dve.drain()
                dve.tensor_copy(hT[:, 0, :, t * P:(t + 1) * P], h32)
                dve.drain()
                dve.tensor_tensor(hT[:, 1, :, t * P:(t + 1) * P], h32, hT[:, 0, :, t * P:(t + 1) * P],
                                  ALU.subtract).then_inc(head_done, 1)

            def qkv(G, g, par):
                for t in range(NT + 2):
                    N = NT * G + t
                    if t < NT:
                        dve.wait_ge(qkv_mm, N + 1)
                        dve.wait_ge(hi2, wait_value(N if t == 0 else N - 1))
                        src = ps_s[0][:, t % 2, 0:GW].rearrange("p (h n) -> p h n", h=HG)
                        bias = bqkv[:, g * GW:(g + 1) * GW].rearrange("p (h n) -> p h n", h=HG)
                        dve.scalar_tensor_tensor(qk32[:, t % 3].rearrange("p (h two) n -> p h (two n)", h=HG),
                                                 src[:, :, 0:2 * HS], 1.0 / W_SCALE, bias[:, :, 0:2 * HS],
                                                 ALU.mult, ALU.add)
                        dve.scalar_tensor_tensor(v32[:, par, t, :].rearrange("p (h n) -> p h n", h=HG),
                                                 src[:, :, 2 * HS:3 * HS], 1.0 / W_SCALE, bias[:, :, 2 * HS:3 * HS],
                                                 ALU.mult, ALU.add).then_inc(qkv_evac, 1)
                    if 1 <= t <= NT:
                        dve.wait_ge(rope_a, N)
                        dve.tensor_tensor(ropeR[:, (t - 1) % 3].rearrange("p h two n -> p (h two) n"),
                                          ropeA[:, (t - 1) % 2], ropeB[:], ALU.add).then_inc(rope_r, 1)
                    if t >= 2:
                        u = (t - 2) % 3
                        dve.tensor_tensor(qk16[:, u, :, 2 * HS:3 * HS], ropeR[:, u, :, 0, :], qk16[:, u, :, 0:HS],
                                          ALU.subtract)
                        dve.tensor_tensor(qk16[:, u, :, R + HS:R + 2 * HS], ropeR[:, u, :, 1, :],
                                          qk16[:, u, :, R:R + HS], ALU.subtract).then_inc(split, 1)
                    dve.drain()
                    if t < NT:
                        swapped = qk32[:, t % 3].rearrange("p n (m two) -> p n m two", two=2)[:, :, :, ::-1]
                        dve.tensor_tensor(ropeB[:].rearrange("p n (m two) -> p n m two", two=2), swapped,
                                          sin_sb[:, t:t + 1, :].rearrange("p o (m two) -> p o m two", two=2).to_broadcast(
                                              [P, 2 * HG, HS // 2, 2]), ALU.mult)
                    if 1 <= t <= NT:
                        u = (t - 1) % 3
                        dve.wait_ge(qk_tr, wait_value(N - 3))
                        dve.tensor_copy(qk16[:, u, :, :].rearrange("p h (two r) -> p h two r", two=2)[:, :, :, 0:HS],
                                        ropeR[:, u])
                    dve.drain()

            def unit_max(h, u, use, n):
                qt, kc = UNITS[u]
                w = min(QC, P * (qt + 1) - QC * kc)
                dve.wait_ge(ring_full, use + 1)
                dve.tensor_reduce(mpart[:, h, qt, kc:kc + 1], ring[n % 2][:, 0:w], AX.X, ALU.max).then_inc(ring_free, 1)

            def maxima(G):
                dve.drain()
                dve.wait_ge(m_tr, wait_value(G))
                dve.tensor_reduce(nmax[:], mpart[:].rearrange("p h t k -> p (h t) k"), AX.X, ALU.max, negate=True)
                dve.drain()
                dve.tensor_scalar(nm16[:, 0, :], nmax[:], 1.0 / M_SCALE, None, ALU.mult)
                dve.drain()
                dve.scalar_tensor_tensor(nm16[:, 1, :], nmax[:], 1.0 / M_SCALE, nm16[:, 0, :], ALU.mult,
                                         ALU.subtract).then_inc(m_split, 1)

            def out_evac(G, cq):
                last_step = NS * G + max(i for i, (q, _) in enumerate(STEPS) if q == cq)
                dve.drain()
                dve.wait_ge(pv_done, last_step + 1)
                dve.reciprocal(onrm[:], ps_d[:])
                dve.drain()
                dve.tensor_tensor(onrm[:], ps_o[:], onrm[:], ALU.mult).then_inc(o_free, 1)
                dve.drain()
                dve.wait_ge(ot_dma[cq % 2], 16 * (NC_ // 2 * G + cq // 2))
                dve.tensor_copy(ot16[:, cq % 2, 0, :], onrm[:])
                dve.drain()
                dve.tensor_tensor(ot16[:, cq % 2, 1, :], onrm[:], ot16[:, cq % 2, 0, :], ALU.subtract).then_inc(ot_split, 1)

            def tail_first(b, t, use, n):
                Z = NT * b + t
                i = t % 2
                dve.wait_ge(ring_full, use + 1)
                dve.wait_ge(out_dma[t % 2], 16 * (NT // 2 * b + t // 2))
                dve.wait_ge(tail_xg, Z + 1)
                dve.tensor_tensor(wk[:, i, :], ring[n % 2][:, :], bc[:, 0, :], ALU.mult).then_inc(ring_free, 1)
                dve.drain()
                dve.tensor_tensor(x1[:, i, :], wk[:, i, :], xs[:, i, :], ALU.add)
                dve.drain()
                dve.bn_stats(stats[:, i, :], x1[:, i, :])
                dve.drain()
                dve.bn_aggr(mv[:, i, :], stats[:, i, :]).then_inc(tail_a, 1)

            def tail_second(b, t):
                i = t % 2
                dve.wait_ge(tail_r1, NT * b + t + 1)
                dve.tensor_scalar(wk[:, i, :], x1[:, i, :], mv[:, i, 0:1], rstd[:, i, :], ALU.subtract, ALU.mult)
                dve.drain()
                dve.tensor_tensor(wk[:, i, :], wk[:, i, :], bc[:, 2, :], ALU.mult)
                dve.drain()
                dve.tensor_tensor(wk[:, i, :], wk[:, i, :], bc[:, 3, :], ALU.add)
                dve.drain()
                dve.bn_stats(stats[:, i, :], wk[:, i, :])
                dve.drain()
                dve.bn_aggr(mv2[:, i, :], stats[:, i, :]).then_inc(tail_c, 1)

            def tail_third(b, t):
                i = t % 2
                dve.wait_ge(tail_r2, NT * b + t + 1)
                dve.wait_ge(tail_xb, NT * b + t + 1)
                dve.tensor_scalar(wk[:, i, :], wk[:, i, :], mv2[:, i, 0:1], rstd2[:, i, :], ALU.subtract, ALU.mult)
                dve.drain()
                dve.tensor_tensor(wk[:, i, :], wk[:, i, :], bc[:, 4, :], ALU.mult)
                dve.drain()
                dve.tensor_tensor(x1[:, i, :], wk[:, i, :], xs[:, i, :], ALU.add).then_inc(tail_e, 1)

            for t in range(NT + 1):
                if t < NT:
                    head_stats(0, t, t // 2)
                if t >= 1:
                    head_evac(0, t - 1, t - 1, t - 1)
                if t < NT:
                    head_normed(0, t)
            dve.wait_ge(misc_ld, 48)
            qkv(0, 0, 0)
            for u in range(NS):
                for h in range(HG):
                    unit_max(h, u, NT + HG * u + h, HG * u + h)
            maxima(0)

            def body(b, first, last):
                jobs = job_base(b)
                base = ring_base(b)
                n = 0
                for g in range(NG):
                    G = NG * b + g
                    nxt = not (last and g == NG - 1)
                    if nxt:
                        qkv(G + 1, (g + 1) % NG, (g + 1) % 2)
                    for s, (cq, kt) in enumerate(STEPS):
                        if nxt:
                            for h in range(HG):
                                unit_max(h, s, base + n, n)
                                n += 1
                        if not first and g in TAIL_STEPS:
                            at = TAIL_STEPS[g]
                            if s in at:
                                tail_first(b - 1, at[s], base + n, n)
                                n += 1
                            if s - 1 in at:
                                tail_second(b - 1, at[s - 1])
                            if s - 2 in at:
                                tail_third(b - 1, at[s - 2])
                        if not last and g in HEAD_STEPS:
                            at = HEAD_STEPS[g]
                            if s in at:
                                head_evac(b + 1, at[s], base + n, n)
                                n += 1
                            if s + 2 in at:
                                head_stats(b + 1, at[s + 2], jobs + (0 if first else NT // 2) + at[s + 2] // 2)
                            if s + 1 in at:
                                head_normed(b + 1, at[s + 1])
                        if s > 0 and STEPS[s - 1][0] != cq:
                            out_evac(G, cq - 1)
                    if nxt:
                        maxima(G + 1)
                    out_evac(G, NC_ - 1)

            batches(dve, body)
            n = NS * HG * (NG - 1) + NT
            for t in range(NT + 1):
                if t < NT:
                    tail_first(B - 1, t, ring_base(B - 1) + n + t, n + t)
                if t >= 1:
                    tail_third(B - 1, t - 1)
                if t < NT:
                    tail_second(B - 1, t)

        @block.tensor
        def _(pe):
            pe.wait_ge(silu_done, 1)
            pe.wait_ge(wm_ld, 16)
            pe.wait_ge(consts, 1)
            for j in range(6):
                if j >= 2:
                    pe.wait_ge(mod_read, j - 1)
                for k in range(KC):
                    mm = pe.matmul(ps_s[j % 2][0:B, 0, :], cT[:, k, :], stage_wmod[:, k, j * C:(j + 1) * C],
                                   start=(k == 0), stop=(k == KC - 1))
                mm.then_inc(mod_mm, 1)

            def head_turn(b, t, use, n):
                pe.wait_ge(head_norm, NT * b + t + 1)
                pe.wait_ge(ring_free, wait_value(use - 1))
                for k in range(KC):
                    mm = pe.transpose(ring[n % 2][:, k * P:(k + 1) * P], wk[:, t % 2, k * P:(k + 1) * P], ident[:])
                mm.then_inc(ring_full, 1)

            def turn_maxima(G):
                pe.wait_ge(m_split, G + 1)
                pe.transpose(ring[0][:, 0:P // 2].bitcast(F16), nm16[:].rearrange("p a n -> p (a n)"),
                             ident16[:]).then_inc(m_tr, 1)

            def qkv(G, g, before):
                for t in range(NT + 3):
                    N = NT * G + t
                    if t < NT:
                        pe.wait_ge(qkv_evac, wait_value(N - 1))
                        i = 0
                        for a, w in ((0, 0), (0, 1), (1, 0)):
                            for k in range(KC):
                                mm = pe.matmul(ps_s[0][:, t % 2, 0:GW], hT[:, a, k, t * P:(t + 1) * P],
                                               w16[:, w, k, g * GW:(g + 1) * GW], start=(i == 0), stop=(i == 3 * KC - 1))
                                i += 1
                        mm.then_inc(qkv_mm, 1)
                    if t == 1 and before is not None:
                        turn_maxima(before)
                    if t >= 3:
                        u = t - 3
                        pe.wait_ge(split, N - 2)
                        pe.wait_ge(hi2, N - 2)
                        pe.wait_ge(tr_evac, wait_value(N - 4))
                        for two in range(2):
                            for h in range(HG):
                                o = (two * HG + h) * P
                                mm = pe.transpose(ps_tr[u % 2][0:R, o:o + P], qk16[:, u % 3, h, two * R:(two + 1) * R],
                                                  ident16[:])
                        mm.then_inc(qk_tr, 1)

            def unit_scores(h, u, par, use, n):
                qt, kc = UNITS[u]
                w = min(QC, P * (qt + 1) - QC * kc)
                diag = kc == qt // TPC
                pe.wait_ge(ring_free, wait_value(use - 1))
                mm = pe.matmul(ring[n % 2][:, 0:w], qk[0:R, par, 0, h, qt * P:(qt + 1) * P],
                               qk[0:R, par, 1, h, kc * QC:kc * QC + w], start=True, stop=not diag)
                if diag:
                    mm = pe.matmul(ring[n % 2][:, w - P:w], identb[:], mask_qk[:], start=False, stop=True)
                mm.then_inc(ring_full, 1)

            def proj(b, t, use, n):
                Z = NT * b + t
                pe.wait_ge(ot_ld[t // 2 % 2], 16 * (NT // 4 * b + t // 4 + 1))
                pe.wait_ge(ring_free, use - 1)
                q = t % 2 * P
                i = 0
                for a, w in ((0, 0), (0, 1), (1, 0)):
                    for k in range(NG):
                        mm = pe.matmul(ring[n % 2][:, :], otin[:, t // 2 % 2, k, a, q:q + P], wp16[:, w, k, :],
                                       start=(i == 0), stop=(i == 3 * NG - 1))
                        i += 1
                mm.then_inc(ring_full, 1)

            def scores(G, par, s):
                cq, kt = STEPS[s]
                q0 = P * max(kt - TPC * cq, 0)
                w = QC - q0
                diag = kt >= TPC * cq
                for p in range(2):
                    pe.wait_ge(exp_done, wait_value(2 * (NS * G + s) + p - 1))
                    for hh in range(2):
                        h = 2 * p + hh
                        mm = pe.matmul(ps_s[p][:, hh, 0:w], qk[0:RM, par, 1, h, kt * P:(kt + 1) * P],
                                       qk[0:RM, par, 0, h, cq * QC + q0:(cq + 1) * QC], start=True, stop=not diag)
                        if diag:
                            mm = pe.matmul(ps_s[p][:, hh, 0:P], identb[:], mask_kq[:], start=False, stop=True)
                    mm.then_inc(st_mm, 1)

            def values(G, par, s):
                cq, kt = STEPS[s]
                q0 = P * max(kt - TPC * cq, 0)
                w = QC - q0
                start, stop = kt == 0, kt == TPC * (cq + 1) - 1
                if start:
                    pe.wait_ge(o_free, wait_value(NC_ * G + cq))
                pe.wait_ge(exp_done, 2 * (NS * G + s) + 2)
                for h in range(HG):
                    pe.matmul(ps_o[h * HS:(h + 1) * HS, q0:QC], v32[:, par, kt, h * HS:(h + 1) * HS],
                              prob[:, s % 2, h // 2, h % 2, 0:w], start=start, stop=stop)
                for h in range(HG):
                    mm = pe.matmul(ps_d[h * HS:(h + 1) * HS, q0:QC], ones[:],
                                   prob[:, s % 2, h // 2, h % 2, 0:w], start=start, stop=stop)
                mm.then_inc(pv_done, 1)

            for t in range(NT):
                head_turn(0, t, t, t)
            pe.wait_ge(wsplit, 1)
            pe.wait_ge(head_done, NT)
            qkv(0, 0, None)
            pe.wait_ge(tr_evac, NT)
            for u in range(NS):
                for h in range(HG):
                    unit_scores(h, u, 0, NT + HG * u + h, HG * u + h)

            def body(b, first, last):
                base = ring_base(b)
                n = 0
                for g in range(NG):
                    G = NG * b + g
                    par = g % 2
                    nxt = not (last and g == NG - 1)
                    if nxt:
                        if g == NG - 1:
                            pe.wait_ge(head_done, NT * (b + 2))
                        qkv(G + 1, (g + 1) % NG, G)
                        pe.wait_ge(qkv_evac, NT * (G + 2))
                        pe.wait_ge(tr_evac, NT * (G + 2))
                    else:
                        turn_maxima(G)
                    pe.wait_ge(m_cp, G + 1)
                    pe.wait_ge(m_dma, 32 * (G + 1))
                    if g == 0:
                        pe.wait_ge(one_rows, 1)
                    for s in range(NS):
                        scores(G, par, s)
                        if nxt:
                            for h in range(HG):
                                unit_scores(h, s, 1 - par, base + n, n)
                                n += 1
                        if not first and g in TAIL_STEPS and s in TAIL_STEPS[g]:
                            proj(b - 1, TAIL_STEPS[g][s], base + n, n)
                            n += 1
                        if not last and g in HEAD_STEPS and s in HEAD_STEPS[g]:
                            head_turn(b + 1, HEAD_STEPS[g][s], base + n, n)
                            n += 1
                        if s > 0:
                            values(G, par, s - 1)
                    values(G, par, NS - 1)

            batches(pe, body)
            n = NS * HG * (NG - 1) + NT
            for t in range(NT):
                proj(B - 1, t, ring_base(B - 1) + n + t, n + t)


_INS = ["L0_attn_x", "L0_attn_W_qkv", "L0_attn_b_qkv", "L0_attn_W_proj", "L0_attn_b_proj", "L0_ffn_ln_g",
        "L0_ffn_ln_b", "L0_c", "L0_wmod"]


def rope_tables(T, HS):
    import numpy as np
    pos = np.arange(T, dtype=np.float32)[:, None]
    i = np.arange(1, HS // 2 + 1, dtype=np.float32)[None]
    theta = np.float32(1.0) / np.float32(10000.0) ** (np.float32(2.0) * (i - np.float32(1.0)) / np.float32(HS))
    ang = pos * theta
    cos = np.repeat(np.cos(ang), 2, axis=1)
    sin = np.repeat(np.sin(ang), 2, axis=1)
    sin[:, 0::2] *= -1
    return cos.astype(np.float32), sin.astype(np.float32)


def kernel(**inputs):
    import numpy as _np
    import concourse.bacc as _bacc
    from concourse import mybir as _mybir
    from concourse.bass_utils import run_bass_kernel_spmd as _run

    nc = _bacc.Bacc("TRN2", target_bir_lowering=False, num_devices=1, dynamic_dma_scratch_size=1024)
    arrays, args = {}, []
    tables = rope_tables(inputs["L0_attn_x"].shape[1], 32)
    named = [(name, inputs[name]) for name in _INS] + [("rope_cos", tables[0]), ("rope_sin", tables[1])]
    for name, value in named:
        a = _np.ascontiguousarray(value)
        arrays[f"in_{name}_dram"] = a
        args.append(nc.dram_tensor(f"in_{name}_dram", a.shape, _mybir.dt.from_np(a.dtype), kind="ExternalInput").ap())
    out = nc.dram_tensor("out_0_dram", inputs["L0_attn_x"].shape, _mybir.dt.float32, kind="ExternalOutput").ap()
    adaln_block_kernel(nc, *args, out)
    r = _run(nc, [arrays], core_ids=[0])
    return r.results[0]["out_0_dram"]
```

```python
from contextlib import ExitStack

import concourse.bass as bass
from concourse import mybir

ALU = mybir.AluOpType
ACT = mybir.ActivationFunctionType
AX = mybir.AxisListType
F32 = mybir.dt.float32
F16 = mybir.dt.float16
BF16 = mybir.dt.bfloat16

P = 128
EPS = 1e-5
W_SCALE = 64.0
M_SCALE = 256.0
MASKED = -1e30


def wait_value(count):
    return max(count, 0) if isinstance(count, int) else count


def adaln_block_kernel(nc, x, w_qkv, b_qkv, w_proj, b_proj, ln_g, ln_b, c, w_mod, rope_cos, rope_sin, out):
    B, T, C = x.shape
    N_QKV = w_qkv.shape[1]
    HS = 32
    H = C // HS
    HG = P // HS
    NG = H // HG
    KC = C // P
    NT = T // P
    QC = 512
    TPC = QC // P
    NC_ = T // QC
    GW = HG * 3 * HS
    R = 3 * HS
    RM = R + 2
    SCALE = float(HS) ** -0.5
    STEPS = [(cq, kt) for cq in range(NC_) for kt in range(TPC * (cq + 1))]
    UNITS = [(qt, kc) for qt in range(NT) for kc in range(qt // TPC + 1)]
    NS = len(STEPS)
    assert len(UNITS) == NS

    PAIRS = [s for s, (cq, kt) in enumerate(STEPS) if kt < TPC * cq and kt % 2 == 0]
    NP = len(PAIRS)
    LEAVE = {cq: max(i for i, (q, _) in enumerate(STEPS) if q == cq) + 1 for cq in range(NC_ - 1)}
    LEAVE[NC_ - 1] = -1

    def leaving(s, stage):
        return next((cq for cq, at in LEAVE.items() if at + stage == s), None)

    T0 = (NT - NT // 3 - 1) // 2
    HEAD_AT = {6 + 2 * k: k for k in range(NT)}
    OWN_AT = {start + 2 * k: TPC * cq + k for cq, start in enumerate((12, 20, 31)) for k in range(TPC)}

    def tail_at(g, first, last):
        if first:
            return {}
        if g < 2:
            return {2 + 8 * k: g * T0 + k for k in range(T0)}
        if g == (2 if last else 3):
            return {2 + 6 * k: 2 * T0 + k for k in range(NT - 2 * T0)}
        return {}

    def head_at(g, last):
        return HEAD_AT if g == 2 and not last else {}

    def own_at(g, last):
        return OWN_AT if g == NG - 1 and last else {}

    RING = NG * NS * HG + 2 * NT

    ot_d = nc.dram_tensor("attn_out_T", (B, P, NG, 2, T), F16, kind="Internal").ap()
    mod_d = nc.dram_tensor("modulation", (B, 8, C), F32, kind="Internal").ap()
    w16_d = nc.dram_tensor("w_qkv_halves", (P, 2, KC, N_QKV), F16, kind="Internal").ap()

    with ExitStack() as ctx:
        def sb(name, shape, dt):
            return ctx.enter_context(nc.sbuf_tensor(name, shape, dt))

        def sem(name):
            return ctx.enter_context(nc.semaphore(name))

        hT = sb("hT", [P, 2, KC, T], F16)
        wg = sb("wg", [P, 2, 2, KC, GW], F16)
        wp16 = sb("wp16", [P, 2, KC, C], F16)
        qk = sb("qk", [P, 2, 2, HG, T], F16)
        v32 = sb("v32", [P, 2, NT, HG * HS], F32)
        prob = sb("prob", [P, 3, 2, 2, QC], F32)
        psum2 = sb("psum2", [P, 2, 2, QC], F32)
        bc = sb("bc", [P, 6, C], F32)
        bg = sb("bg", [P, 2, GW], F32)
        cos_sb = sb("cos_sb", [P, NT, HS // 2], F32)
        sin_sb = sb("sin_sb", [P, NT, HS], F32)
        xs = sb("xs", [P, 2, C], F32)
        wk = sb("wk", [P, 2, C], F32)
        x1 = sb("x1", [P, 2, C], F32)
        otin = sb("otin", [P, 2, NG, 2, 2 * P], F16)
        qk32 = sb("qk32", [P, 3, 2 * HG, HS], F32)
        ropeA = sb("ropeA", [P, 2, 2 * HG, HS], F32)
        ropeB = sb("ropeB", [P, 2 * HG, HS], F32)
        ropeR = qk32[:].rearrange("p s (h two) n -> p s h two n", two=2)
        qk16 = sb("qk16", [P, 3, HG, 2 * R], F16)
        osum = sb("osum", [P, QC], F32)
        dsum = sb("dsum", [P, QC], F32)
        ot16 = sb("ot16", [P, 2, QC], F16)
        mpart = sb("mpart", [P, HG, NT, NC_], F32)
        nmax = sb("nmax", [P, HG * NT], F32)
        nm16 = sb("nm16", [P, 2, HG * NT], F16)
        mrow = sb("mrow", [P, P], F16)
        ident = sb("ident", [P, P], F32)
        ident16 = sb("ident16", [P, P], F16)
        identb = sb("identb", [P, P], BF16)
        mask_qk = sb("mask_qk", [P, P], BF16)
        mask_kq = sb("mask_kq", [P, P], BF16)
        ones = sb("ones", [P, HS], F32)
        cT = sb("cT", [P, KC, B], F32)
        eT = sb("eT", [P, KC, B], F32)
        colmod = sb("colmod", [P, 2, KC], F32)
        stats = sb("stats", [P, 2, 6], F32)
        mv = sb("mv", [P, 2, 2], F32)
        mv2 = sb("mv2", [P, 2, 2], F32)
        rstd = sb("rstd", [P, 2, 1], F32)
        rstd2 = sb("rstd2", [P, 2, 1], F32)
        vare = sb("vare", [P, 2, 1], F32)
        neg_half = sb("neg_half", [P, 1], F32)
        eps_t = sb("eps_t", [P, 1], F32)

        stage_w = hT[:].rearrange("p a k t -> p (a k t)").bitcast(F32)
        stage_wqkv = stage_w[:, 0:KC * N_QKV].rearrange("p (k n) -> p k n", k=KC)
        stage_wproj = stage_w[:, KC * N_QKV:KC * (N_QKV + C)].rearrange("p (k n) -> p k n", k=KC)
        stage_wmod = qk[:].rearrange("p a b h t -> p (a b h t)").bitcast(F32)[:, 0:KC * 6 * C].rearrange(
            "p (k n) -> p k n", k=KC)
        stage_w16 = prob[:].rearrange("p a b h q -> p (a b h q)").bitcast(F16).rearrange(
            "p (a k n) -> p a k n", a=2, k=KC)
        rows = qk[:].rearrange("p a b h t -> p (a b h t)").bitcast(F32)[0:B, KC * 6 * C:(KC * 6 + 8) * C].rearrange(
            "p (m n) -> p m n", n=C)
        prow = v32[:].rearrange("p a t n -> p (a t n)")[0:B, 0:5 * C].rearrange("p (m n) -> p m n", n=C)

        ps_s = [ctx.enter_context(nc.psum_tensor(f"ps_s{i}", [P, 2, QC], F32)) for i in range(2)]
        ps_o = ctx.enter_context(nc.psum_tensor("ps_o", [P, QC], F32))
        ps_d = ctx.enter_context(nc.psum_tensor("ps_d", [P, QC], F32))
        ring = [ctx.enter_context(nc.psum_tensor(f"ring{i}", [P, QC], F32)) for i in range(2)]
        ps_tr = [ps_s[1][:, i, :].bitcast(F16) for i in range(2)]

        c_ld, w_ld, wm_ld, row_ld, misc_ld = (sem(n) for n in ("c_ld", "w_ld", "wm_ld", "row_ld", "misc_ld"))
        consts, wsplit, silu_e, silu_done, mod_mm, mod_row = (
            sem(n) for n in ("consts", "wsplit", "silu_e", "silu_done", "mod_mm", "mod_row"))
        mod_read, wproj_split, w_st, ot_dma = (
            sem(n) for n in ("mod_read", "wproj_split", "w_st", "ot_dma"))
        mod_st, col_ld, bc_ld, one_rows = (sem(n) for n in ("mod_st", "col_ld", "bc_ld", "one_rows"))
        x_ld, ot_ld, out_dma, wg_ld = ([sem(f"{n}{i}") for i in range(2)] 
                                             for n in ("x_ld", "ot_ld", "out_dma", "wg_ld"))
        head_stat, head_rstd, head_norm, head_hi, head_done = (
            sem(n) for n in ("head_stat", "head_rstd", "head_norm", "head_hi", "head_done"))
        qkv_mm, qkv_evac, rope_a, rope_r, hi2, split, qk_tr, tr_evac = (
            sem(n) for n in ("qkv_mm", "qkv_evac", "rope_a", "rope_r", "hi2", "split", "qk_tr", "tr_evac"))
        ring_full, ring_free = sem("ring_full"), sem("ring_free")
        m_split, m_tr, m_cp, m_dma = (sem(n) for n in ("m_split", "m_tr", "m_cp", "m_dma"))
        st_mm, exp_done, pv_done, pair_sum, pair_used = (
            sem(n) for n in ("st_mm", "exp_done", "pv_done", "pair_sum", "pair_used"))
        o_free, o_rcp, o_norm, o_hi, ot_split = (sem(n) for n in ("o_free", "o_rcp", "o_norm", "o_hi", "ot_split"))
        tail_xg, tail_x1, tail_a, tail_r1, tail_xb, tail_n1, tail_h1, tail_c, tail_r2, tail_n2, tail_e = (
            sem(n) for n in ("tail_xg", "tail_x1", "tail_a", "tail_r1", "tail_xb", "tail_n1", "tail_h1", "tail_c",
                             "tail_r2", "tail_n2", "tail_e"))

        def job_base(b):
            return NT // 2 if isinstance(b, int) and b == 0 else NT * b

        def ring_base(b):
            prologue = NT + NS * HG
            return prologue if isinstance(b, int) and b == 0 else prologue + RING * b - NT

        def batches(eng, body):
            body(0, first=True, last=False)
            with eng.Fori(1, B - 1) as b:
                body(b, first=False, last=False)
            return body(B - 1, first=False, last=True)

        block = ctx.enter_context(nc.Block())

        @block.sync
        def _(sp):
            def load_x(b, t):
                sp.wait_ge(mod_st, 16)
                sp.dma_start(xs[:, t % 2, :], x[b, t * P:(t + 1) * P, :]).then_inc(x_ld[t % 2], 16)

            def load_columns(b):
                with nc.allow_non_contiguous_dma(reason="a batch's columns of the modulation, 1024 words"):
                    for i in range(2):
                        sp.dma_start(colmod[:, i, :], mod_d[b, i, :].rearrange("(k p) -> p k", p=P)).then_inc(col_ld, 16)

            def load_group(g):
                sp.dma_start(wg[:, g % 2].rearrange("p a k n -> p (a k) n"), w16_d[:, :, :, g * GW:(g + 1) * GW].rearrange(
                    "p a k n -> p (a k) n")).then_inc(wg_ld[g % 2], 16)
                sp.dma_start(bg[:, g % 2, :], b_qkv[g * GW:(g + 1) * GW].rearrange("(a n) -> a n", a=1).to_broadcast(
                    [P, GW])).then_inc(wg_ld[g % 2], 16)

            with nc.allow_non_contiguous_dma(reason="c transposed, 2048 words"):
                for k in range(KC):
                    sp.dma_start(cT[:, k, :], c[:, k * P:(k + 1) * P].rearrange("b p -> p b")).then_inc(c_ld, 16)
            sp.dma_start(stage_wmod, w_mod.rearrange("(k p) n -> p k n", p=P)).then_inc(wm_ld, 16)
            sp.dma_start(stage_wqkv, w_qkv.rearrange("(k p) n -> p k n", p=P)).then_inc(w_ld, 16)
            sp.dma_start(stage_wproj, w_proj.rearrange("(k p) n -> p k n", p=P)).then_inc(w_ld, 16)
            for t in range(2):
                sp.dma_start(xs[:, t, :], x[0, t * P:(t + 1) * P, :]).then_inc(x_ld[t], 16)
            for i, row in enumerate((b_proj, ln_g, ln_b)):
                sp.dma_start(prow[:, i, :], row.rearrange("(a n) -> a n", a=1).to_broadcast([B, C])).then_inc(row_ld, 16)
            sp.dma_start(cos_sb[:], rope_cos.rearrange("(t p) n -> p t n", p=P)).then_inc(misc_ld, 16)
            sp.dma_start(sin_sb[:], rope_sin.rearrange("(t p) n -> p t n", p=P)).then_inc(misc_ld, 16)
            sp.wait_ge(wsplit, 1)
            sp.dma_start(w16_d, stage_w16).then_inc(w_st, 16)
            sp.wait_ge(mod_row, 1)
            sp.dma_start(mod_d, rows).then_inc(mod_st, 16)
            sp.wait_ge(mod_st, 16)
            load_columns(0)
            sp.wait_ge(w_st, 16)
            for g in range(2):
                load_group(g)
            for t in range(2, NT):
                sp.wait_ge(head_norm, t - 1)
                load_x(0, t)

            def maxima_rows(G, par):
                sp.wait_ge(m_cp, G + 1)
                for i in range(2):
                    sp.dma_start(qk[R + i:R + i + 1, par, 0, :, :].rearrange("p h (t q) -> p (h t) q", q=P),
                                 mrow[i * HG * NT:(i + 1) * HG * NT, :]).then_inc(m_dma, 16)

            def tail_loads(b, t, xs_use, count):
                Z = NT * b + t
                if t == 0:
                    sp.wait_ge(tail_e, wait_value(Z))
                    sp.wait_ge(mod_st, 16)
                    sp.dma_start(bc[:], mod_d[b, 2:8, :].rearrange("(a m) n -> a m n", a=1).to_broadcast(
                        [P, 6, C])).then_inc(bc_ld, 16)
                if t % TPC == 0:
                    cq = t // TPC
                    sp.wait_ge(ot_dma, 16 * (NG * NC_ * (b + 1) - NC_ + cq + 1))
                if t % 2 == 0:
                    if t >= 4:
                        sp.wait_ge(tail_a, Z - 2)
                    sp.wait_ge(mod_st, 16)
                    sp.dma_start(otin[:, t // 2 % 2], ot_d[b, :, :, :, t * P:(t + 2) * P]).then_inc(ot_ld[t // 2 % 2], 16)
                sp.wait_ge(xs_use, count)
                load_x(b, t)

            def store_out(b, t):
                sp.wait_ge(tail_e, NT * b + t + 1)
                sp.wait_ge(mod_st, 16)
                sp.dma_start(out[b, t * P:(t + 1) * P, :], x1[:, t % 2, :]).then_inc(out_dma[t % 2], 16)

            def body(b, first, last):
                for g in range(NG):
                    maxima_rows(NG * b + g, g % 2)
                    if not (last and g >= NG - 2):
                        sp.wait_ge(qkv_evac, NT * (NG * b + g + 1))
                        load_group((g + 2) % NG)
                    tail, head, own = tail_at(g, first, last), head_at(g, last), own_at(g, last)
                    for s in range(NS):
                        cq = leaving(s, 5)
                        if cq == NC_ - 1 and g == 0 and not first:
                            store_ot(b - 1, NG - 1, cq)
                        elif cq is not None and not (cq == NC_ - 1 and g == 0):
                            store_ot(b, g - (cq == NC_ - 1), cq)
                        if s + 2 in tail:
                            t = tail[s + 2]
                            Z = NT * (b - 1) + t
                            if t < 2 or (t < 2 * T0 + 2 and t >= 2 * T0 and not last):
                                tail_loads(b - 1, t, head_norm, NT * (b + 1 + (t > 1)))
                            else:
                                tail_loads(b - 1, t, tail_e, Z - 1)
                        if s - 5 in tail:
                            store_out(b - 1, tail[s - 5])
                        if s + 2 in own:
                            tail_loads(b, own[s + 2], tail_e, NT * b + own[s + 2] - 1)
                        if s - 2 in own:
                            store_out(b, own[s - 2])
                        if s == 0 and head:
                            load_columns(b + 1)
                        if s + 5 in head:
                            t = head[s + 5]
                            if t >= 2 or first:
                                sp.wait_ge(head_norm, NT * (b + 1) + t - 1)
                            elif t == 0:
                                sp.wait_ge(tail_e, NT * (b - 1) + 2 * T0)
                            load_x(b + 1, t)

            def store_ot(b, g, cq):
                sp.wait_ge(ot_split, NC_ * (NG * b + g) + cq + 1)
                sp.wait_ge(mod_st, 16)
                sp.dma_start(ot_d[b, :, g, :, cq * QC:(cq + 1) * QC], ot16[:]).then_inc(ot_dma, 16)

            batches(sp, body)
            store_ot(B - 1, NG - 1, NC_ - 1)
            for t in range(len(OWN_AT), NT):
                tail_loads(B - 1, t, tail_e, NT * (B - 1) + t - 1)
                if t > len(OWN_AT):
                    store_out(B - 1, t - 1)
            store_out(B - 1, NT - 1)
            for i in range(2):
                sp.wait_ge(out_dma[i], 16 * B * NT // 2)

        @block.gpsimd
        def _(pool):
            pool.memset(ident[:], 0.0)
            pool.memset(ident16[:], 0.0)
            pool.memset(identb[:], 0.0)
            pool.memset(mask_qk[:], 0.0)
            pool.memset(mask_kq[:], 0.0)
            pool.memset(ones[:], 1.0)
            pool.memset(neg_half[:], -0.5)
            pool.memset(eps_t[:], EPS)
            pool.drain()
            for one in (ident, ident16, identb):
                pool.affine_select(out=one[:], in_=one[:], compare_op=ALU.not_equal, fill=1.0, base=0,
                                   pattern=[[-1, P]], channel_multiplier=1)
            pool.affine_select(out=mask_qk[:], in_=mask_qk[:], compare_op=ALU.is_ge, fill=MASKED, base=0,
                               pattern=[[-1, P]], channel_multiplier=1)
            pool.affine_select(out=mask_kq[:], in_=mask_kq[:], compare_op=ALU.is_ge, fill=MASKED, base=0,
                               pattern=[[1, P]], channel_multiplier=-1)
            pool.drain().then_inc(consts, 1)

            def inv_std(dst, src):
                pool.tensor_tensor(vare[:, 0, :], src[:, 1:2], eps_t[:], ALU.add)
                pool.drain()
                return pool.tensor_tensor(dst, vare[:, 0, :], neg_half[:], ALU.pow)

            def head_tile(b, t):
                pool.wait_ge(head_stat, NT * b + t + 1)
                inv_std(rstd[:, t % 2, :], mv[:, t % 2, :]).then_inc(head_rstd, 1)

            def rope_tile(G, t):
                N = NT * G + t
                pool.wait_ge(qkv_evac, N + 1)
                pool.wait_ge(rope_r, wait_value(N - 1))
                pool.tensor_tensor(
                    ropeA[:, t % 2].rearrange("p n (m two) -> p n m two", two=2),
                    qk32[:, t % 3].rearrange("p n (m two) -> p n m two", two=2),
                    cos_sb[:, t:t + 1, :].rearrange("p o (m one) -> p o m one", one=1).to_broadcast(
                        [P, 2 * HG, HS // 2, 2]), ALU.mult).then_inc(rope_a, 1)

            def head_low(b, t):
                pool.wait_ge(head_hi, NT * b + t + 1)
                pool.tensor_tensor(hT[:, 1, :, t * P:(t + 1) * P], x1[:, t % 2, :].rearrange("p (k q) -> p k q", k=KC),
                                   hT[:, 0, :, t * P:(t + 1) * P], ALU.subtract).then_inc(head_done, 1)

            def add_pair(G, j):
                s = PAIRS[j]
                for p in range(2):
                    pool.wait_ge(exp_done, 2 * (NS * G + s + 1) + p + 1)
                    pool.wait_ge(pair_used, wait_value(NP * G + j))
                    pool.tensor_tensor(psum2[:, p], prob[:, s % 3, p], prob[:, (s + 1) % 3, p],
                                       ALU.add).then_inc(pair_sum, 1)

            def out_norm(G, cq):
                pool.wait_ge(o_rcp, 2 * (NC_ * G + cq) + 2)
                pool.tensor_tensor(osum[:], osum[:], dsum[:], ALU.mult).then_inc(o_norm, 1)

            def out_low(G, cq):
                pool.wait_ge(o_hi, NC_ * G + cq + 1)
                pool.tensor_tensor(ot16[:, 1, :], osum[:], ot16[:, 0, :],
                                   ALU.subtract).then_inc(ot_split, 1)

            def tail_x(b, t, job):
                if t == 0:
                    pool.wait_ge(bc_ld, 16 * (b + 1))
                pool.wait_ge(x_ld[t % 2], 16 * (job + 1))
                pool.tensor_tensor(xs[:, t % 2, :], xs[:, t % 2, :], bc[:, 1, :], ALU.add).then_inc(tail_xg, 1)

            def tail_stage(b, t, stage, use, job):
                Z = NT * b + t
                i = t % 2
                if stage == 0:
                    tail_x(b, t, job)
                    pool.drain()
                    pool.wait_ge(ring_free, use + 1)
                    pool.wait_ge(out_dma[i], 16 * (NT // 2 * b + t // 2))
                    pool.tensor_tensor(x1[:, i, :], wk[:, i, :], xs[:, i, :], ALU.add).then_inc(tail_x1, 1)
                elif stage == 1:
                    tail_1(b, t)
                elif stage == 2:
                    pool.wait_ge(tail_n1, Z + 1)
                    pool.tensor_tensor(wk[:, i, :], wk[:, i, :], bc[:, 2, :], ALU.mult)
                    pool.drain()
                    pool.tensor_tensor(wk[:, i, :], wk[:, i, :], bc[:, 3, :], ALU.add).then_inc(tail_h1, 1)
                elif stage == 3:
                    tail_2(b, t)
                else:
                    pool.wait_ge(tail_n2, Z + 1)
                    pool.tensor_tensor(wk[:, i, :], wk[:, i, :], bc[:, 4, :], ALU.mult)
                    pool.drain()
                    pool.tensor_tensor(x1[:, i, :], wk[:, i, :], xs[:, i, :], ALU.add).then_inc(tail_e, 1)
                pool.drain()

            def tail_1(b, t):
                pool.wait_ge(tail_a, NT * b + t + 1)
                inv_std(rstd[:, t % 2, :], mv[:, t % 2, :]).then_inc(tail_r1, 1)
                pool.tensor_tensor(xs[:, t % 2, :], x1[:, t % 2, :], bc[:, 5, :], ALU.add).then_inc(tail_xb, 1)

            def tail_2(b, t):
                pool.drain()
                pool.wait_ge(tail_c, NT * b + t + 1)
                inv_std(rstd2[:, t % 2, :], mv2[:, t % 2, :]).then_inc(tail_r2, 1)

            for t in range(NT + 1):
                if t < NT:
                    pool.drain()
                    head_tile(0, t)
                if t >= 1:
                    head_low(0, t - 1)
            pool.wait_ge(misc_ld, 32)
            for t in range(NT):
                rope_tile(0, t)

            def body(b, first, last):
                jobs = job_base(b)
                n = 0
                for g in range(NG):
                    G = NG * b + g
                    nxt = not (last and g == NG - 1)
                    if nxt:
                        for t in range(NT):
                            rope_tile(G + 1, t)
                    pool.drain()
                    tail, head, own = tail_at(g, first, last), head_at(g, last), own_at(g, last)
                    uses = {}
                    for s in range(NS):
                        if nxt:
                            n += HG
                        if s in tail:
                            uses[tail[s]] = ring_base(b) + n
                        n += (s in tail) + (s in head) + (s in own)
                        if s - 1 in PAIRS:
                            add_pair(G, PAIRS.index(s - 1))
                        for stage in range(5):
                            if s - stage in tail:
                                t = tail[s - stage]
                                job = jobs + t // 2 + (NT // 2 if t >= 2 * T0 and not last else 0)
                                tail_stage(b - 1, t, stage, uses[t], job)
                        if s in own:
                            tail_x(b, own[s], jobs + NT // 2 + own[s] // 2)
                            tail_1(b, own[s])
                        if s - 1 in own:
                            tail_2(b, own[s - 1])
                            pool.drain()
                        if s + 2 in head:
                            head_tile(b + 1, head[s + 2])
                            pool.drain()
                        if s in head:
                            head_low(b + 1, head[s])
                        for stage, out_stage in ((2, out_norm), (4, out_low)):
                            cq = leaving(s, stage)
                            if cq is not None and not (cq == NC_ - 1 and g == 0 and first):
                                out_stage(G - (cq == NC_ - 1), cq)

            batches(pool, body)
            out_norm(NG * B - 1, NC_ - 1)
            out_low(NG * B - 1, NC_ - 1)
            for t in range(len(OWN_AT), NT):
                pool.drain()
                tail_x(B - 1, t, NT * (2 * B - 1) // 2 + t // 2)
                tail_1(B - 1, t)
                tail_2(B - 1, t)

        @block.scalar
        def _(act):
            act.wait_ge(c_ld, 16 * KC)
            act.activation(eT[:], cT[:], ACT.Exp, scale=-1.0).then_inc(silu_e, 1)

            def second_hi(G, t):
                N = NT * G + t
                act.wait_ge(rope_r, N + 1)
                act.wait_ge(qk_tr, wait_value(N - 2))
                act.copy(qk16[:, t % 3, :, HS:2 * HS], ropeR[:, t % 3, :, 0, :])
                act.copy(qk16[:, t % 3, :, R + 2 * HS:R + 3 * HS], ropeR[:, t % 3, :, 1, :]).then_inc(hi2, 1)

            def transposed(G, par, t):
                act.wait_ge(qk_tr, NT * G + t + 1)
                act.copy(qk[0:R, par, :, :, t * P:(t + 1) * P].rearrange("p two h q -> p (two h) q"),
                         ps_tr[t % 2][0:R, :].rearrange("p (n q) -> p n q", q=P)).then_inc(tr_evac, 1)

            def qkv(G, par):
                for t in range(NT + 3):
                    if t < NT:
                        second_hi(G, t)
                    if t >= 3:
                        transposed(G, par, t - 3)

            def maxima(G):
                act.wait_ge(m_tr, G + 1)
                act.wait_ge(m_dma, 32 * G)
                act.copy(mrow[:], ring[0][:, 0:P // 2].bitcast(F16)).then_inc(m_cp, 1)

            qkv(0, 0)

            def body(b, first, last):
                for g in range(NG):
                    G = NG * b + g
                    maxima(G)
                    if not (last and g == NG - 1):
                        qkv(G + 1, (g + 1) % 2)
                    for s, (cq, kt) in enumerate(STEPS):
                        w = QC - P * max(kt - TPC * cq, 0)
                        S = NS * G + s
                        for p in range(2):
                            act.wait_ge(st_mm, 2 * S + p + 1)
                            act.wait_ge(pv_done, wait_value(S - 2 if s >= 3 else NS * G))
                            if s < 3:
                                act.wait_ge(pair_sum, wait_value(2 * NP * G))
                            elif s - 3 in PAIRS or s - 4 in PAIRS:
                                j = PAIRS.index(s - 3 if s - 3 in PAIRS else s - 4)
                                act.wait_ge(pair_sum, 2 * (NP * G + j) + p + 1)
                            act.activation(prob[:, s % 3, p, :, 0:w], ps_s[p][:, :, 0:w], ACT.Exp,
                                           scale=SCALE).then_inc(exp_done, 1)
                        out = leaving(s, 0)
                        if out is not None:
                            leave(G, out)
                        out = leaving(s, 3)
                        if out is not None and not (out == NC_ - 1 and g == 0 and first):
                            out_high(G - (out == NC_ - 1), out)
                    leave(G, NC_ - 1)

            def leave(G, cq):
                last_step = NS * G + max(i for i, (q, _) in enumerate(STEPS) if q == cq)
                act.wait_ge(pv_done, last_step + 1)
                act.wait_ge(ot_split, wait_value(NC_ * G + cq))
                act.copy(dsum[:], ps_d[:])
                act.copy(osum[:], ps_o[:]).then_inc(o_free, 1)

            def out_high(G, cq):
                act.wait_ge(o_norm, NC_ * G + cq + 1)
                act.wait_ge(ot_dma, wait_value(16 * (NC_ * G + cq)))
                act.copy(ot16[:, 0, :], osum[:]).then_inc(o_hi, 1)

            batches(act, body)
            out_high(NG * B - 1, NC_ - 1)

        @block.vector
        def _(dve):
            dve.wait_ge(silu_e, 1)
            dve.tensor_scalar(eT[:], eT[:], 1.0, None, ALU.add)
            dve.drain()
            dve.reciprocal(eT[:], eT[:])
            dve.drain()
            dve.tensor_tensor(cT[:], cT[:], eT[:], ALU.mult).then_inc(silu_done, 1)
            dve.wait_ge(w_ld, 32)
            for st in (stage_wqkv, stage_wproj):
                dve.tensor_scalar(st, st, W_SCALE, None, ALU.mult)
            dve.drain()
            for st, dst in ((stage_wqkv, stage_w16), (stage_wproj, wp16)):
                dve.tensor_copy(dst[:, 0], st)
            dve.drain()
            dve.tensor_tensor(stage_w16[:, 1], stage_wqkv, stage_w16[:, 0], ALU.subtract).then_inc(wsplit, 1)
            dve.tensor_tensor(wp16[:, 1], stage_wproj, wp16[:, 0], ALU.subtract).then_inc(wproj_split, 1)
            dve.wait_ge(row_ld, 48)
            for j in range(6):
                dve.wait_ge(mod_mm, j + 1)
                src = ps_s[j % 2][0:B, 0, :]
                gate = prow[:, 3, :]
                sign = prow[:, 4, :]
                if j == 0:
                    dve.tensor_copy(rows[:, 0, :], src)
                elif j == 1:
                    dve.tensor_scalar(rows[:, 1, :], src, 1.0, None, ALU.add)
                elif j == 3:
                    dve.tensor_copy(rows[:, 5, :], src)
                elif j == 4:
                    dve.tensor_scalar(rows[:, 4, :], src, 1.0, None, ALU.add)
                else:
                    dve.tensor_copy(gate, src)
                    dve.drain()
                    dve.tensor_scalar(sign, gate, 0.0, 2.0, ALU.is_ge, ALU.mult)
                    dve.tensor_scalar(rows[:, 7, :], gate, -1.0, None, ALU.mult)
                    dve.drain()
                    dve.tensor_tensor(gate, gate, rows[:, 7, :], ALU.max)
                    dve.tensor_scalar(sign, sign, -1.0, None, ALU.add)
                    dve.drain()
                    dve.tensor_scalar(gate, gate, 0.25, None, ALU.max)
                    dve.drain()
                    dve.tensor_tensor(gate, gate, sign, ALU.mult)
                    dve.drain()
                    if j == 2:
                        dve.tensor_scalar(rows[:, 2, :], gate, 1.0 / W_SCALE, None, ALU.mult)
                        dve.tensor_tensor(rows[:, 3, :], gate, prow[:, 0, :], ALU.mult)
                    else:
                        dve.tensor_tensor(rows[:, 6, :], gate, prow[:, 1, :], ALU.mult)
                        dve.tensor_tensor(rows[:, 7, :], gate, prow[:, 2, :], ALU.mult)
                dve.drain().then_inc(mod_read, 1)
            dve.drain().then_inc(mod_row, 1)
            for par in range(2):
                dve.memset(qk[R:RM, par, 1, :, :], M_SCALE)
            dve.memset(mpart[:], -3e38)
            dve.drain().then_inc(one_rows, 1)

            def head_stats(b, t, job):
                dve.wait_ge(x_ld[t % 2], 16 * (job + 1))
                dve.wait_ge(head_rstd, wait_value(NT * b + t - 1))
                dve.bn_stats(stats[:, t % 2, :], xs[:, t % 2, :])
                dve.drain()
                dve.bn_aggr(mv[:, t % 2, :], stats[:, t % 2, :]).then_inc(head_stat, 1)

            def head_normed(b, t):
                dve.wait_ge(head_rstd, NT * b + t + 1)
                dve.tensor_scalar(wk[:, t % 2, :], xs[:, t % 2, :], mv[:, t % 2, 0:1], rstd[:, t % 2, :],
                                  ALU.subtract, ALU.mult).then_inc(head_norm, 1)

            def head_evac(b, t, use, n):
                if t == 0:
                    dve.wait_ge(col_ld, 32 * (b + 1))
                    for i in range(2):
                        dve.wait_ge(out_dma[i], wait_value(16 * (NT // 2 * (b - 2) + T0)))
                dve.wait_ge(head_done, wait_value(NT * b + t - 1))
                dve.wait_ge(ring_full, use + 1)
                h32 = x1[:, t % 2, :].rearrange("p (k q) -> p k q", k=KC)
                src = ring[n % 2][:, :].rearrange("p (k q) -> p k q", k=KC)
                for k in range(KC):
                    normed = dve.tensor_scalar(h32[:, k, :], src[:, k, :], colmod[:, 1, k:k + 1], colmod[:, 0, k:k + 1],
                                               ALU.mult, ALU.add)
                normed.then_inc(ring_free, 1)
                dve.drain()
                dve.tensor_copy(hT[:, 0, :, t * P:(t + 1) * P], h32).then_inc(head_hi, 1)

            def qkv(G, g, par):
                for t in range(NT + 2):
                    N = NT * G + t
                    if t < NT:
                        dve.wait_ge(qkv_mm, N + 1)
                        dve.wait_ge(hi2, wait_value(N if t == 0 else N - 1))
                        src = ps_s[0][:, t % 2, 0:GW].rearrange("p (h n) -> p h n", h=HG)
                        bias = bg[:, par, :].rearrange("p (h n) -> p h n", h=HG)
                        dve.scalar_tensor_tensor(qk32[:, t % 3].rearrange("p (h two) n -> p h (two n)", h=HG),
                                                 src[:, :, 0:2 * HS], 1.0 / W_SCALE, bias[:, :, 0:2 * HS],
                                                 ALU.mult, ALU.add)
                        dve.scalar_tensor_tensor(v32[:, par, t, :].rearrange("p (h n) -> p h n", h=HG),
                                                 src[:, :, 2 * HS:3 * HS], 1.0 / W_SCALE, bias[:, :, 2 * HS:3 * HS],
                                                 ALU.mult, ALU.add).then_inc(qkv_evac, 1)
                    if 1 <= t <= NT:
                        dve.wait_ge(rope_a, N)
                        dve.tensor_tensor(ropeR[:, (t - 1) % 3].rearrange("p h two n -> p (h two) n"),
                                          ropeA[:, (t - 1) % 2], ropeB[:], ALU.add).then_inc(rope_r, 1)
                    if t >= 2:
                        u = (t - 2) % 3
                        dve.tensor_tensor(qk16[:, u, :, 2 * HS:3 * HS], ropeR[:, u, :, 0, :], qk16[:, u, :, 0:HS],
                                          ALU.subtract)
                        dve.tensor_tensor(qk16[:, u, :, R + HS:R + 2 * HS], ropeR[:, u, :, 1, :],
                                          qk16[:, u, :, R:R + HS], ALU.subtract).then_inc(split, 1)
                    dve.drain()
                    if t < NT:
                        swapped = qk32[:, t % 3].rearrange("p n (m two) -> p n m two", two=2)[:, :, :, ::-1]
                        dve.tensor_tensor(ropeB[:].rearrange("p n (m two) -> p n m two", two=2), swapped,
                                          sin_sb[:, t:t + 1, :].rearrange("p o (m two) -> p o m two", two=2).to_broadcast(
                                              [P, 2 * HG, HS // 2, 2]), ALU.mult)
                    if 1 <= t <= NT:
                        u = (t - 1) % 3
                        dve.wait_ge(qk_tr, wait_value(N - 3))
                        dve.tensor_copy(qk16[:, u, :, :].rearrange("p h (two r) -> p h two r", two=2)[:, :, :, 0:HS],
                                        ropeR[:, u])
                    dve.drain()

            def unit_max(h, u, use, n):
                qt, kc = UNITS[u]
                w = min(QC, P * (qt + 1) - QC * kc)
                dve.wait_ge(ring_full, use + 1)
                dve.tensor_reduce(mpart[:, h, qt, kc:kc + 1], ring[n % 2][:, 0:w], AX.X, ALU.max).then_inc(ring_free, 1)

            def maxima(G):
                dve.drain()
                dve.wait_ge(m_tr, wait_value(G))
                dve.tensor_reduce(nmax[:], mpart[:].rearrange("p h t k -> p (h t) k"), AX.X, ALU.max, negate=True)
                dve.drain()
                dve.tensor_scalar(nm16[:, 0, :], nmax[:], 1.0 / M_SCALE, None, ALU.mult)
                dve.drain()
                dve.scalar_tensor_tensor(nm16[:, 1, :], nmax[:], 1.0 / M_SCALE, nm16[:, 0, :], ALU.mult,
                                         ALU.subtract).then_inc(m_split, 1)

            def out_reciprocal(G, cq, half):
                dve.wait_ge(o_free, NC_ * G + cq + 1)
                cols = slice(half * QC // 2, (half + 1) * QC // 2)
                dve.reciprocal(dsum[:, cols], dsum[:, cols]).then_inc(o_rcp, 1)

            def tail_stage(b, t, stage, use, n):
                Z = NT * b + t
                i = t % 2
                if stage == 0:
                    dve.wait_ge(ring_full, use + 1)
                    if t >= 2:
                        dve.wait_ge(tail_e, Z - 1)
                    dve.tensor_tensor(wk[:, i, :], ring[n % 2][:, :], bc[:, 0, :], ALU.mult).then_inc(ring_free, 1)
                elif stage == 1:
                    dve.wait_ge(tail_x1, Z + 1)
                    dve.bn_stats(stats[:, i, :], x1[:, i, :])
                    dve.drain()
                    dve.bn_aggr(mv[:, i, :], stats[:, i, :]).then_inc(tail_a, 1)
                elif stage == 2:
                    dve.wait_ge(tail_r1, Z + 1)
                    dve.tensor_scalar(wk[:, i, :], x1[:, i, :], mv[:, i, 0:1], rstd[:, i, :], ALU.subtract,
                                      ALU.mult).then_inc(tail_n1, 1)
                elif stage == 3:
                    dve.wait_ge(tail_h1, Z + 1)
                    dve.bn_stats(stats[:, i, :], wk[:, i, :])
                    dve.drain()
                    dve.bn_aggr(mv2[:, i, :], stats[:, i, :]).then_inc(tail_c, 1)
                else:
                    dve.wait_ge(tail_r2, Z + 1)
                    dve.tensor_scalar(wk[:, i, :], wk[:, i, :], mv2[:, i, 0:1], rstd2[:, i, :], ALU.subtract,
                                      ALU.mult).then_inc(tail_n2, 1)

            def tail_first(b, t, use, n):
                Z = NT * b + t
                i = t % 2
                dve.wait_ge(ring_full, use + 1)
                dve.wait_ge(out_dma[t % 2], 16 * (NT // 2 * b + t // 2))
                dve.wait_ge(tail_xg, Z + 1)
                dve.tensor_tensor(wk[:, i, :], ring[n % 2][:, :], bc[:, 0, :], ALU.mult).then_inc(ring_free, 1)
                dve.drain()
                dve.tensor_tensor(x1[:, i, :], wk[:, i, :], xs[:, i, :], ALU.add)
                dve.drain()
                dve.bn_stats(stats[:, i, :], x1[:, i, :])
                dve.drain()
                dve.bn_aggr(mv[:, i, :], stats[:, i, :]).then_inc(tail_a, 1)

            def tail_second(b, t):
                i = t % 2
                dve.wait_ge(tail_r1, NT * b + t + 1)
                dve.tensor_scalar(wk[:, i, :], x1[:, i, :], mv[:, i, 0:1], rstd[:, i, :], ALU.subtract, ALU.mult)
                dve.drain()
                dve.tensor_tensor(wk[:, i, :], wk[:, i, :], bc[:, 2, :], ALU.mult)
                dve.drain()
                dve.tensor_tensor(wk[:, i, :], wk[:, i, :], bc[:, 3, :], ALU.add)
                dve.drain()
                dve.bn_stats(stats[:, i, :], wk[:, i, :])
                dve.drain()
                dve.bn_aggr(mv2[:, i, :], stats[:, i, :]).then_inc(tail_c, 1)

            def tail_third(b, t):
                i = t % 2
                dve.wait_ge(tail_r2, NT * b + t + 1)
                dve.wait_ge(tail_xb, NT * b + t + 1)
                dve.tensor_scalar(wk[:, i, :], wk[:, i, :], mv2[:, i, 0:1], rstd2[:, i, :], ALU.subtract, ALU.mult)
                dve.drain()
                dve.tensor_tensor(wk[:, i, :], wk[:, i, :], bc[:, 4, :], ALU.mult)
                dve.drain()
                dve.tensor_tensor(x1[:, i, :], wk[:, i, :], xs[:, i, :], ALU.add).then_inc(tail_e, 1)

            for t in range(NT + 1):
                if t < NT:
                    head_stats(0, t, t // 2)
                if t >= 1:
                    head_evac(0, t - 1, t - 1, t - 1)
                if t < NT:
                    head_normed(0, t)
            dve.wait_ge(misc_ld, 32)
            qkv(0, 0, 0)
            for u in range(NS):
                for h in range(HG):
                    unit_max(h, u, NT + HG * u + h, HG * u + h)
            maxima(0)

            def body(b, first, last):
                jobs = job_base(b)
                base = ring_base(b)
                n = 0
                for g in range(NG):
                    G = NG * b + g
                    nxt = not (last and g == NG - 1)
                    if nxt:
                        qkv(G + 1, (g + 1) % NG, (g + 1) % 2)
                    tail, head, own = tail_at(g, first, last), head_at(g, last), own_at(g, last)
                    for s in range(NS):
                        if nxt:
                            for h in range(HG):
                                unit_max(h, s, base + n, n)
                                n += 1
                        for stage in range(5):
                            if s - stage in tail:
                                tail_stage(b - 1, tail[s - stage], stage, base + n, n)
                        n += s in tail
                        if s in own:
                            tail_first(b, own[s], base + n, n)
                            n += 1
                        if s - 1 in own:
                            tail_second(b, own[s - 1])
                        if s - 2 in own:
                            tail_third(b, own[s - 2])
                        if s in head:
                            head_evac(b + 1, head[s], base + n, n)
                            n += 1
                        if s + 2 in head:
                            first_job = jobs if first else jobs + T0
                            head_stats(b + 1, head[s + 2], first_job + head[s + 2] // 2)
                        if s + 1 in head:
                            head_normed(b + 1, head[s + 1])
                        for half in range(2):
                            cq = leaving(s, 1 + half)
                            if cq is not None and not (cq == NC_ - 1 and g == 0 and first):
                                out_reciprocal(G - (cq == NC_ - 1), cq, half)
                    if nxt:
                        maxima(G + 1)
                return n

            n = batches(dve, body)
            for half in range(2):
                out_reciprocal(NG * B - 1, NC_ - 1, half)
            for t in range(len(OWN_AT), NT + 1):
                if t < NT:
                    tail_first(B - 1, t, ring_base(B - 1) + n, n)
                    n += 1
                if t > len(OWN_AT):
                    tail_third(B - 1, t - 1)
                if t < NT:
                    tail_second(B - 1, t)

        @block.tensor
        def _(pe):
            pe.wait_ge(silu_done, 1)
            pe.wait_ge(wm_ld, 16)
            pe.wait_ge(consts, 1)
            for j in range(6):
                if j >= 2:
                    pe.wait_ge(mod_read, j - 1)
                for k in range(KC):
                    mm = pe.matmul(ps_s[j % 2][0:B, 0, :], cT[:, k, :], stage_wmod[:, k, j * C:(j + 1) * C],
                                   start=(k == 0), stop=(k == KC - 1))
                mm.then_inc(mod_mm, 1)

            def head_turn(b, t, use, n):
                pe.wait_ge(head_norm, NT * b + t + 1)
                pe.wait_ge(ring_free, wait_value(use - 1))
                for k in range(KC):
                    mm = pe.transpose(ring[n % 2][:, k * P:(k + 1) * P], wk[:, t % 2, k * P:(k + 1) * P], ident[:])
                mm.then_inc(ring_full, 1)

            def turn_maxima(G):
                pe.wait_ge(m_split, G + 1)
                pe.transpose(ring[0][:, 0:P // 2].bitcast(F16), nm16[:].rearrange("p a n -> p (a n)"),
                             ident16[:]).then_inc(m_tr, 1)

            def qkv(G, g, before, loads):
                pe.wait_ge(wg_ld[g % 2], loads)
                for t in range(NT + 3):
                    N = NT * G + t
                    if t < NT:
                        pe.wait_ge(qkv_evac, wait_value(N - 1))
                        i = 0
                        for a, w in ((0, 0), (0, 1), (1, 0)):
                            for k in range(KC):
                                mm = pe.matmul(ps_s[0][:, t % 2, 0:GW], hT[:, a, k, t * P:(t + 1) * P],
                                               wg[:, g % 2, w, k, :], start=(i == 0), stop=(i == 3 * KC - 1))
                                i += 1
                        mm.then_inc(qkv_mm, 1)
                    if t == 1 and before is not None:
                        turn_maxima(before)
                    if t >= 3:
                        u = t - 3
                        pe.wait_ge(split, N - 2)
                        pe.wait_ge(hi2, N - 2)
                        pe.wait_ge(tr_evac, wait_value(N - 4))
                        for two in range(2):
                            for h in range(HG):
                                o = (two * HG + h) * P
                                mm = pe.transpose(ps_tr[u % 2][0:R, o:o + P], qk16[:, u % 3, h, two * R:(two + 1) * R],
                                                  ident16[:])
                        mm.then_inc(qk_tr, 1)

            def unit_scores(h, u, par, use, n):
                qt, kc = UNITS[u]
                w = min(QC, P * (qt + 1) - QC * kc)
                diag = kc == qt // TPC
                pe.wait_ge(ring_free, wait_value(use - 1))
                mm = pe.matmul(ring[n % 2][:, 0:w], qk[0:R, par, 0, h, qt * P:(qt + 1) * P],
                               qk[0:R, par, 1, h, kc * QC:kc * QC + w], start=True, stop=not diag)
                if diag:
                    mm = pe.matmul(ring[n % 2][:, w - P:w], identb[:], mask_qk[:], start=False, stop=True)
                mm.then_inc(ring_full, 1)

            def proj(b, t, use, n):
                if t == 0:
                    pe.wait_ge(wproj_split, 1)
                pe.wait_ge(ot_ld[t // 2 % 2], 16 * (NT // 4 * b + t // 4 + 1))
                pe.wait_ge(ring_free, use - 1)
                q = t % 2 * P
                i = 0
                for a, w in ((0, 0), (0, 1), (1, 0)):
                    for k in range(NG):
                        mm = pe.matmul(ring[n % 2][:, :], otin[:, t // 2 % 2, k, a, q:q + P], wp16[:, w, k, :],
                                       start=(i == 0), stop=(i == 3 * NG - 1))
                        i += 1
                mm.then_inc(ring_full, 1)

            def scores(G, par, s, p):
                cq, kt = STEPS[s]
                q0 = P * max(kt - TPC * cq, 0)
                w = QC - q0
                diag = kt >= TPC * cq
                pe.wait_ge(exp_done, wait_value(2 * (NS * G + s) + p - 1))
                for hh in range(2):
                    h = 2 * p + hh
                    mm = pe.matmul(ps_s[p][:, hh, 0:w], qk[0:RM, par, 1, h, kt * P:(kt + 1) * P],
                                   qk[0:RM, par, 0, h, cq * QC + q0:(cq + 1) * QC], start=True, stop=not diag)
                    if diag:
                        mm = pe.matmul(ps_s[p][:, hh, 0:P], identb[:], mask_kq[:], start=False, stop=True)
                mm.then_inc(st_mm, 1)

            def values(G, par, s):
                cq, kt = STEPS[s]
                q0 = P * max(kt - TPC * cq, 0)
                if kt == 0:
                    pe.wait_ge(o_free, wait_value(NC_ * G + cq))
                pe.wait_ge(exp_done, 2 * (NS * G + s) + 2)
                for h in range(HG):
                    mm = pe.matmul(ps_o[h * HS:(h + 1) * HS, q0:QC], v32[:, par, kt, h * HS:(h + 1) * HS],
                                   prob[:, s % 3, h // 2, h % 2, 0:QC - q0], start=kt == 0,
                                   stop=kt == TPC * (cq + 1) - 1)
                if kt < TPC * cq:
                    mm.then_inc(pv_done, 1)

            def denominators(G, s):
                cq, kt = STEPS[s]
                if s - 2 in PAIRS:
                    j = PAIRS.index(s - 2)
                    for h in range(HG):
                        if h % 2 == 0:
                            pe.wait_ge(pair_sum, 2 * (NP * G + j) + h // 2 + 1)
                        mm = pe.matmul(ps_d[h * HS:(h + 1) * HS, :], ones[:], psum2[:, h // 2, h % 2, :],
                                       start=kt == 2, stop=False)
                    mm.then_inc(pair_used, 1)
                if kt >= TPC * cq:
                    q0 = P * (kt - TPC * cq)
                    for h in range(HG):
                        mm = pe.matmul(ps_d[h * HS:(h + 1) * HS, q0:QC], ones[:],
                                       prob[:, s % 3, h // 2, h % 2, 0:QC - q0], start=kt == 0,
                                       stop=kt == TPC * (cq + 1) - 1)
                    mm.then_inc(pv_done, 1)

            for t in range(NT):
                head_turn(0, t, t, t)
            pe.wait_ge(head_done, NT)
            qkv(0, 0, None, 32)
            pe.wait_ge(tr_evac, NT)
            for u in range(NS):
                for h in range(HG):
                    unit_scores(h, u, 0, NT + HG * u + h, HG * u + h)

            def body(b, first, last):
                base = ring_base(b)
                n = 0
                for g in range(NG):
                    G = NG * b + g
                    par = g % 2
                    nxt = not (last and g == NG - 1)
                    if nxt:
                        if g == NG - 1:
                            pe.wait_ge(head_done, NT * (b + 2))
                        qkv(G + 1, (g + 1) % NG, G, 32 * (NG // 2 * b + (g + 1) // 2 + 1))
                        pe.wait_ge(qkv_evac, NT * (G + 2))
                        pe.wait_ge(tr_evac, NT * (G + 2))
                    else:
                        turn_maxima(G)
                    pe.wait_ge(m_cp, G + 1)
                    pe.wait_ge(m_dma, 32 * (G + 1))
                    if g == 0:
                        pe.wait_ge(one_rows, 1)
                    tail, head, own = tail_at(g, first, last), head_at(g, last), own_at(g, last)
                    for s in range(NS + 1):
                        if s < NS:
                            scores(G, par, s, 0)
                            if nxt:
                                unit_scores(0, s, 1 - par, base + n, n)
                            scores(G, par, s, 1)
                            if nxt:
                                unit_scores(1, s, 1 - par, base + n + 1, n + 1)
                        if s > 0:
                            values(G, par, s - 1)
                        if s < NS and nxt:
                            unit_scores(2, s, 1 - par, base + n + 2, n + 2)
                        if s > 0:
                            denominators(G, s - 1)
                        if s < NS and nxt:
                            unit_scores(3, s, 1 - par, base + n + 3, n + 3)
                            n += HG
                        if s in tail or s in own:
                            proj(b if s in own else b - 1, own[s] if s in own else tail[s], base + n, n)
                            n += 1
                        if s in head:
                            head_turn(b + 1, head[s], base + n, n)
                            n += 1
                return n

            n = batches(pe, body)
            for t in range(len(OWN_AT), NT):
                proj(B - 1, t, ring_base(B - 1) + n, n)
                n += 1


_INS = ["L0_attn_x", "L0_attn_W_qkv", "L0_attn_b_qkv", "L0_attn_W_proj", "L0_attn_b_proj", "L0_ffn_ln_g",
        "L0_ffn_ln_b", "L0_c", "L0_wmod"]


def rope_tables(T, HS):
    import numpy as np
    pos = np.arange(T, dtype=np.float32)[:, None]
    i = np.arange(1, HS // 2 + 1, dtype=np.float32)[None]
    theta = np.float32(1.0) / np.float32(10000.0) ** (np.float32(2.0) * (i - np.float32(1.0)) / np.float32(HS))
    ang = pos * theta
    cos = np.cos(ang)
    sin = np.repeat(np.sin(ang), 2, axis=1)
    sin[:, 0::2] *= -1
    return cos.astype(np.float32), sin.astype(np.float32)


def kernel(**inputs):
    import numpy as _np
    import concourse.bacc as _bacc
    from concourse import mybir as _mybir
    from concourse.bass_utils import run_bass_kernel_spmd as _run

    nc = _bacc.Bacc("TRN2", target_bir_lowering=False, num_devices=1, dynamic_dma_scratch_size=1024)
    arrays, args = {}, []
    tables = rope_tables(inputs["L0_attn_x"].shape[1], 32)
    named = [(name, inputs[name]) for name in _INS] + [("rope_cos", tables[0]), ("rope_sin", tables[1])]
    for name, value in named:
        a = _np.ascontiguousarray(value)
        arrays[f"in_{name}_dram"] = a
        args.append(nc.dram_tensor(f"in_{name}_dram", a.shape, _mybir.dt.from_np(a.dtype), kind="ExternalInput").ap())
    out = nc.dram_tensor("out_0_dram", inputs["L0_attn_x"].shape, _mybir.dt.float32, kind="ExternalOutput").ap()
    adaln_block_kernel(nc, *args, out)
    r = _run(nc, [arrays], core_ids=[0])
    return r.results[0]["out_0_dram"]
```

```python
from contextlib import ExitStack

import concourse.bass as bass
from concourse import mybir

ALU = mybir.AluOpType
ACT = mybir.ActivationFunctionType
AX = mybir.AxisListType
F32 = mybir.dt.float32
F16 = mybir.dt.float16
BF16 = mybir.dt.bfloat16

P = 128
EPS = 1e-5
W_SCALE = 64.0
M_SCALE = 256.0
MASKED = -1e30


def wait_value(count):
    return max(count, 0) if isinstance(count, int) else count


def adaln_block_kernel(nc, x, w_qkv, b_qkv, w_proj, b_proj, ln_g, ln_b, c, w_mod, rope_cos, rope_sin, out):
    B, T, C = x.shape
    N_QKV = w_qkv.shape[1]
    HS = 32
    H = C // HS
    HG = P // HS
    NG = H // HG
    KC = C // P
    NT = T // P
    QC = 512
    TPC = QC // P
    NC_ = T // QC
    GW = HG * 3 * HS
    R = 3 * HS
    RM = R + 2
    SCALE = float(HS) ** -0.5
    STEPS = [(cq, kt) for cq in range(NC_) for kt in range(TPC * (cq + 1))]
    UNITS = [(qt, kc) for qt in range(NT) for kc in range(qt // TPC + 1)]
    NS = len(STEPS)
    assert len(UNITS) == NS

    PAIRS = [s for s, (cq, kt) in enumerate(STEPS) if kt < TPC * cq and kt % 2 == 0]
    NP = len(PAIRS)
    LEAVE = {cq: max(i for i, (q, _) in enumerate(STEPS) if q == cq) + 1 for cq in range(NC_ - 1)}
    LEAVE[NC_ - 1] = -1
    FAST = {"leave": 0, 0: 1, 1: 1, 2: 2, 3: 2, "norm": 2, "high": 3, "low": 4, "store": 5}
    LATE = {0: 2, 1: 2, 2: 3, 3: 3, "norm": 3, "high": 4, "low": 4, "store": 5}
    SLOW = {"leave": 0, 0: 1, 1: 2, 2: 3, 3: 4, "norm": 4, "high": 5, "low": 6, "store": 7}

    def leaving(s, stage, own):
        for cq, at in LEAVE.items():
            steps = LATE if cq == NC_ - 1 else FAST if own else SLOW
            if stage in steps and at + steps[stage] == s:
                return cq
        return None

    T0 = (NT - NT // 3 - 1) // 2
    HEAD_AT = {6 + 2 * k: k for k in range(NT)}
    OWN_AT = {start + 2 * k: TPC * cq + k for cq, start in enumerate((12, 20, 31)) for k in range(TPC)}

    LATE_TURNS = {(0, 1): NT - 3, (0, 3): NT - 2, (1, 1): NT - 1}

    def tail_at(g, first, last):
        if first:
            return {}
        if g < 2:
            return {s: g * T0 + k for k, s in enumerate((2, 8, 16, 24, 30))}
        if g == (2 if last else 3):
            return {s: 2 * T0 + k for k, s in enumerate((2, 8, 14, 20, 26, 30))}
        return {}

    def head_at(g, last):
        return HEAD_AT if g == 2 and not last else {}

    def own_at(g, last):
        return OWN_AT if g == NG - 1 and last else {}

    def product_load(s, tail, head):
        def width(s):
            cq, kt = STEPS[s]
            return (TPC - max(kt - TPC * cq, 0)) / TPC
        load = 4 * width(s)
        if s > 0:
            load += 4.2 * width(s - 1)
            if STEPS[s - 1][1] >= TPC * STEPS[s - 1][0]:
                load += 4.2 * width(s - 1)
        return load + 4.2 * (s - 3 in PAIRS) + 6 * (s in tail) + 2 * (s in head)

    def vector_load(s, tail, head):
        load = 2.4 * sum(leaving(s, part, False) is not None for part in range(TPC))
        load += sum(c * (s - at in tail) for at, c in ((0, 1.7), (2, 2.2), (4, 4), (6, 2.2), (8, 4)))
        return load + 2.7 * (s in head) + 2.2 * (s + 2 in head) + (s + 1 in head)

    def unit_plan(tail, head):
        fits = lambda r: [min(5, max(0, r * product_load(s, tail, head) - vector_load(s, tail, head))) for s in range(NS)]
        r = 0.0
        while sum(fits(r)) < NS * HG:
            r += 0.01
        plan, k, done = [], 0, 0.0
        for room in fits(r):
            done += room
            upto = min(NS * HG, k + 5, int(done + 0.5))
            plan.append([(i // HG, i % HG) for i in range(k, upto)])
            k = upto
        assert k == NS * HG
        return plan

    RING = NG * NS * HG + 2 * NT

    ot_d = nc.dram_tensor("attn_out_T", (B, P, NG, 2, T), F16, kind="Internal").ap()
    mod_d = nc.dram_tensor("modulation", (B, 8, C), F32, kind="Internal").ap()
    w16_d = nc.dram_tensor("w_qkv_halves", (P, 2, KC, N_QKV), F16, kind="Internal").ap()

    with ExitStack() as ctx:
        def sb(name, shape, dt):
            return ctx.enter_context(nc.sbuf_tensor(name, shape, dt))

        def sem(name):
            return ctx.enter_context(nc.semaphore(name))

        hT = sb("hT", [P, 2, KC, T], F16)
        wg = sb("wg", [P, 2, 2, KC, GW], F16)
        wp16 = sb("wp16", [P, 2, KC, C], F16)
        qk = sb("qk", [P, 2, 2, HG, T], F16)
        v32 = sb("v32", [P, 2, NT, HG * HS], F32)
        prob = sb("prob", [P, 3, 2, 2, QC], F32)
        psum2 = sb("psum2", [P, 2, 2, QC], F32)
        bc = sb("bc", [P, 6, C], F32)
        bg = sb("bg", [P, 2, GW], F32)
        cos_sb = sb("cos_sb", [P, NT, HS // 2], F32)
        sin_sb = sb("sin_sb", [P, NT, HS], F32)
        xs = sb("xs", [P, 2, C], F32)
        wk = sb("wk", [P, 2, C], F32)
        x1 = sb("x1", [P, 2, C], F32)
        otin = sb("otin", [P, 2, NG, 2, 2 * P], F16)
        qk32 = sb("qk32", [P, 3, 2 * HG, HS], F32)
        ropeA = sb("ropeA", [P, 2, 2 * HG, HS], F32)
        ropeB = sb("ropeB", [P, 2 * HG, HS], F32)
        ropeR = qk32[:].rearrange("p s (h two) n -> p s h two n", two=2)
        qk16 = sb("qk16", [P, 3, HG, 2 * R], F16)
        osum = sb("osum", [P, QC], F32)
        dsum = sb("dsum", [P, QC], F32)
        ot16 = sb("ot16", [P, 2, QC], F16)
        mpart = sb("mpart", [P, HG, NT, NC_], F32)
        nmax = sb("nmax", [P, HG * NT], F32)
        nm16 = sb("nm16", [P, 2, HG * NT], F16)
        mrow = sb("mrow", [P, P], F16)
        ident = sb("ident", [P, P], F32)
        ident16 = sb("ident16", [P, P], F16)
        identb = sb("identb", [P, P], BF16)
        mask_qk = sb("mask_qk", [P, P], BF16)
        mask_kq = sb("mask_kq", [P, P], BF16)
        ones = sb("ones", [P, HS], F32)
        cT = sb("cT", [P, KC, B], F32)
        eT = sb("eT", [P, KC, B], F32)
        colmod = sb("colmod", [P, 2, KC], F32)
        stats = sb("stats", [P, 2, 6], F32)
        mv = sb("mv", [P, 2, 2], F32)
        mv2 = sb("mv2", [P, 2, 2], F32)
        rstd = sb("rstd", [P, 2, 1], F32)
        rstd2 = sb("rstd2", [P, 2, 1], F32)
        vare = sb("vare", [P, 2, 1], F32)
        neg_half = sb("neg_half", [P, 1], F32)
        eps_t = sb("eps_t", [P, 1], F32)

        stage_w = hT[:].rearrange("p a k t -> p (a k t)").bitcast(F32)
        stage_wqkv = stage_w[:, 0:KC * N_QKV].rearrange("p (k n) -> p k n", k=KC)
        stage_wproj = stage_w[:, KC * N_QKV:KC * (N_QKV + C)].rearrange("p (k n) -> p k n", k=KC)
        stage_wmod = qk[:].rearrange("p a b h t -> p (a b h t)").bitcast(F32)[:, 0:KC * 6 * C].rearrange(
            "p (k n) -> p k n", k=KC)
        stage_w16 = prob[:].rearrange("p a b h q -> p (a b h q)").bitcast(F16).rearrange(
            "p (a k n) -> p a k n", a=2, k=KC)
        rows = qk[:].rearrange("p a b h t -> p (a b h t)").bitcast(F32)[0:B, KC * 6 * C:(KC * 6 + 8) * C].rearrange(
            "p (m n) -> p m n", n=C)
        prow = v32[:].rearrange("p a t n -> p (a t n)")[0:B, 0:5 * C].rearrange("p (m n) -> p m n", n=C)

        end_x = psum2[:].rearrange("p a h q -> p (a h) q")
        end_wk, end_x1 = (prob[:].rearrange("p a b h q -> p (a b h) q")[:, TPC * i:TPC * (i + 1), :] for i in range(2))

        def tail_buffers(b, t):
            if isinstance(b, int) and b == B - 1 and t >= NT - TPC:
                i = t - (NT - TPC)
                return end_x[:, i, :], end_wk[:, i, :], end_x1[:, i, :]
            return xs[:, t % 2, :], wk[:, t % 2, :], x1[:, t % 2, :]

        NBK = 3
        ps_scores = [ctx.enter_context(nc.psum_tensor(f"ps_scores{i}", [P, QC], F32)) for i in range(NBK)]
        ps_out = ctx.enter_context(nc.psum_tensor("ps_out", [P, QC], F32))
        ps_den = ctx.enter_context(nc.psum_tensor("ps_den", [P, QC], F32))
        ring = [ctx.enter_context(nc.psum_tensor(f"ring{i}", [P, QC], F32)) for i in range(NBK)]
        SHIFT = -NT % NBK
        mod_banks = ps_scores + [ps_out, ps_den, ring[2]]
        ps_tr = [bank[:].bitcast(F16) for bank in (ps_out, ps_den)]

        c_ld, w_ld, wm_ld, row_ld, rope_ld = (sem(n) for n in ("c_ld", "w_ld", "wm_ld", "row_ld", "rope_ld"))
        w_hi, wqkv_split, wproj_split, w_st = (sem(n) for n in ("w_hi", "wqkv_split", "wproj_split", "w_st"))
        consts, silu_e, silu_done, mod_mm, mod_row, mod_st, scale_rows = (
            sem(n) for n in ("consts", "silu_e", "silu_done", "mod_mm", "mod_row", "mod_st", "scale_rows"))
        turn_done, turn_free = sem("turn_done"), sem("turn_free")
        col_ld, bc_ld, ot_dma = (sem(n) for n in ("col_ld", "bc_ld", "ot_dma"))
        x_ld, ot_ld, out_dma, wg_ld = ([sem(f"{n}{i}") for i in range(2)]
                                       for n in ("x_ld", "ot_ld", "out_dma", "wg_ld"))
        head_stat, head_rstd, head_norm, head_scaled, head_hi, head_done = (
            sem(n) for n in ("head_stat", "head_rstd", "head_norm", "head_scaled", "head_hi", "head_done"))
        qkv_mm, qkv_evac, rope_a, rope_r, hi2_done, lo_done, qk_tr, tr_evac = (
            sem(n) for n in ("qkv_mm", "qkv_evac", "rope_a", "rope_r", "hi2_done", "lo_done", "qk_tr", "tr_evac"))
        ring_full, ring_free = sem("ring_full"), sem("ring_free")
        max_split, max_turned, max_rows, max_dma = (
            sem(n) for n in ("max_split", "max_turned", "max_rows", "max_dma"))
        scores_done, exp_done, prob_used, pair_sum, pair_used = (
            sem(n) for n in ("scores_done", "exp_done", "prob_used", "pair_sum", "pair_used"))
        sums_left, recip_done, out_normed, out_hi, out_split, end_split = (
            sem(n) for n in ("sums_left", "recip_done", "out_normed", "out_hi", "out_split", "end_split"))
        tail_x_bias, tail_x1_sum, tail_stats1, tail_rstd1, tail_x1_shift, tail_stats2, tail_rstd2, tail_done = (
            sem(n) for n in ("tail_x_bias", "tail_x1_sum", "tail_stats1", "tail_rstd1", "tail_x1_shift",
                             "tail_stats2", "tail_rstd2", "tail_done"))

        def job_base(b):
            return NT // 2 if isinstance(b, int) and b == 0 else NT * b

        def ring_base(b):
            return NS * HG if isinstance(b, int) and b == 0 else NS * HG + RING * b - NT

        def ring_first(b):
            return ring_base(b if isinstance(b, int) and b == 0 else 1) % NBK

        assert RING % NBK == 0

        def batches(eng, body):
            body(0, first=True, last=False)
            with eng.Fori(1, B - 1) as b:
                body(b, first=False, last=False)
            return body(B - 1, first=False, last=True)

        block = ctx.enter_context(nc.Block())

        @block.sync
        def _(sp):
            def load_x(b, t, to=None):
                if not isinstance(b, int):
                    sp.wait_ge(mod_st, 32)
                sp.dma_start(xs[:, t % 2, :] if to is None else to, x[b, t * P:(t + 1) * P, :]).then_inc(x_ld[t % 2], 16)

            def load_columns(b):
                with nc.allow_non_contiguous_dma(reason="a batch's columns of the modulation, 1024 words"):
                    for i in range(2):
                        sp.dma_start(colmod[:, i, :], mod_d[b, i, :].rearrange("(k p) -> p k", p=P)).then_inc(col_ld, 16)

            def load_group(g):
                sp.dma_start(wg[:, g % 2].rearrange("p a k n -> p (a k) n"), w16_d[:, :, :, g * GW:(g + 1) * GW].rearrange(
                    "p a k n -> p (a k) n")).then_inc(wg_ld[g % 2], 16)
                sp.dma_start(bg[:, g % 2, :], b_qkv[g * GW:(g + 1) * GW].rearrange("(a n) -> a n", a=1).to_broadcast(
                    [P, GW])).then_inc(wg_ld[g % 2], 16)

            with nc.allow_non_contiguous_dma(reason="c transposed, 2048 words"):
                for k in range(KC):
                    sp.dma_start(cT[:, k, :], c[:, k * P:(k + 1) * P].rearrange("b p -> p b")).then_inc(c_ld, 16)
            sp.dma_start(stage_wqkv, w_qkv.rearrange("(k p) n -> p k n", p=P)).then_inc(w_ld, 16)
            sp.dma_start(stage_wproj, w_proj.rearrange("(k p) n -> p k n", p=P)).then_inc(w_ld, 16)
            sp.dma_start(stage_wmod, w_mod.rearrange("(k p) n -> p k n", p=P)).then_inc(wm_ld, 16)
            for t in range(2):
                sp.dma_start(xs[:, t, :], x[0, t * P:(t + 1) * P, :]).then_inc(x_ld[t], 16)
            for i, row in enumerate((b_proj, ln_g, ln_b)):
                sp.dma_start(prow[:, i, :], row.rearrange("(a n) -> a n", a=1).to_broadcast([B, C])).then_inc(row_ld, 16)
            sp.dma_start(cos_sb[:], rope_cos.rearrange("(t p) n -> p t n", p=P)).then_inc(rope_ld, 16)
            sp.dma_start(sin_sb[:], rope_sin.rearrange("(t p) n -> p t n", p=P)).then_inc(rope_ld, 16)
            sp.wait_ge(wqkv_split, 1)
            sp.dma_start(w16_d, stage_w16).then_inc(w_st, 16)
            sp.wait_ge(mod_row, 1)
            sp.dma_start(mod_d[:, 0:2, :], rows[:, 0:2, :]).then_inc(mod_st, 16)
            sp.wait_ge(mod_st, 16)
            load_columns(0)
            for t in range(2, NT):
                sp.wait_ge(head_norm, t - 1)
                load_x(0, t)
                if t == 3:
                    sp.wait_ge(w_st, 16)
                    for g in range(2):
                        load_group(g)
                    sp.wait_ge(mod_row, 2)
                    sp.dma_start(mod_d[:, 2:8, :], rows[:, 2:8, :]).then_inc(mod_st, 16)
            sp.wait_ge(mod_st, 32)

            def maxima_rows(G, par):
                sp.wait_ge(max_rows, G + 1)
                for i in range(2):
                    sp.dma_start(qk[R + i:R + i + 1, par, 0, :, :].rearrange("p h (t q) -> p (h t) q", q=P),
                                 mrow[i * HG * NT:(i + 1) * HG * NT, :]).then_inc(max_dma, 16)

            def tail_loads(b, t, xs_use, count):
                Z = NT * b + t
                if t == 0:
                    sp.wait_ge(tail_done, wait_value(Z))
                    sp.wait_ge(mod_st, 32)
                    sp.dma_start(bc[:], mod_d[b, 2:8, :].rearrange("(a m) n -> a m n", a=1).to_broadcast(
                        [P, 6, C])).then_inc(bc_ld, 16)
                if t % TPC == 0:
                    cq = t // TPC
                    sp.wait_ge(ot_dma, 16 * (NG * NC_ * (b + 1) - NC_ + cq + 1))
                if t % 2 == 0:
                    if t >= 4:
                        sp.wait_ge(tail_stats1, Z - 2)
                    sp.wait_ge(mod_st, 32)
                    sp.dma_start(otin[:, t // 2 % 2], ot_d[b, :, :, :, t * P:(t + 2) * P]).then_inc(ot_ld[t // 2 % 2], 16)
                sp.wait_ge(xs_use, count)
                load_x(b, t)

            def store_out(b, t):
                sp.wait_ge(tail_done, NT * b + t + 1)
                sp.wait_ge(mod_st, 32)
                sp.dma_start(out[b, t * P:(t + 1) * P, :], tail_buffers(b, t)[2]).then_inc(out_dma[t % 2], 16)

            def end_attention(t):
                sp.wait_ge(tail_stats1, NT * (B - 1) + t - 2)
                sp.dma_start(otin[:, t // 2 % 2, 0:NG - 1], ot_d[B - 1, :, 0:NG - 1, :, t * P:(t + 2) * P]).then_inc(
                    ot_ld[t // 2 % 2], 16)

            def body(b, first, last):
                for g in range(NG):
                    maxima_rows(NG * b + g, g % 2)
                    if not (last and g >= NG - 2):
                        sp.wait_ge(qkv_evac, NT * (NG * b + g + 1))
                        load_group((g + 2) % NG)
                    tail, head, own = tail_at(g, first, last), head_at(g, last), own_at(g, last)
                    for s in range(NS):
                        cq = leaving(s, "store", bool(own))
                        if cq == NC_ - 1 and g == 0 and not first:
                            store_ot(b - 1, NG - 1, cq)
                        elif cq is not None and not (cq == NC_ - 1 and g == 0):
                            store_ot(b, g - (cq == NC_ - 1), cq)
                        if s + 2 in tail:
                            t = tail[s + 2]
                            Z = NT * (b - 1) + t
                            if t < 2 or (t < 2 * T0 + 2 and t >= 2 * T0 and not last):
                                tail_loads(b - 1, t, head_norm, NT * (b + 1 + (t > 1)))
                            else:
                                tail_loads(b - 1, t, tail_done, Z - 1)
                        if s - 9 in tail:
                            store_out(b - 1, tail[s - 9])
                        if s + 2 in own:
                            tail_loads(b, own[s + 2], tail_done, NT * b + own[s + 2] - 1)
                        if s - 2 in own:
                            store_out(b, own[s - 2])
                        if own and s == NS - 2:
                            sp.wait_ge(pair_used, NP * (NG * B - 1))
                            sp.wait_ge(tail_x_bias, NT * B - TPC)
                            for t in range(NT - TPC, NT):
                                load_x(B - 1, t, end_x[:, t - (NT - TPC), :])
                            end_attention(NT - TPC)
                        if s == 0 and head:
                            load_columns(b + 1)
                        if s + 5 in head:
                            t = head[s + 5]
                            if t >= 2 or first:
                                sp.wait_ge(head_norm, NT * (b + 1) + t - 1)
                            elif t == 0:
                                sp.wait_ge(tail_done, NT * (b - 1) + 2 * T0)
                            load_x(b + 1, t)

            def store_ot(b, g, cq):
                sp.wait_ge(out_split, NC_ * (NG * b + g) + cq + 1)
                sp.wait_ge(mod_st, 32)
                sp.dma_start(ot_d[b, :, g, :, cq * QC:(cq + 1) * QC], ot16[:]).then_inc(ot_dma, 16)

            batches(sp, body)
            end_attention(NT - 2)
            for t in range(NT - TPC, NT):
                store_out(B - 1, t)
            for i in range(2):
                sp.wait_ge(out_dma[i], 16 * B * NT // 2)

        @block.gpsimd
        def _(pool):
            pool.memset(ident[:], 0.0)
            pool.memset(ident16[:], 0.0)
            pool.memset(identb[:], 0.0)
            pool.memset(mask_qk[:], 0.0)
            pool.memset(mask_kq[:], 0.0)
            pool.memset(ones[:], 1.0)
            pool.memset(neg_half[:], -0.5)
            pool.memset(eps_t[:], EPS)
            pool.drain()
            for one in (ident, ident16, identb):
                pool.affine_select(out=one[:], in_=one[:], compare_op=ALU.not_equal, fill=1.0, base=0,
                                   pattern=[[-1, P]], channel_multiplier=1)
            pool.affine_select(out=mask_qk[:], in_=mask_qk[:], compare_op=ALU.is_ge, fill=MASKED, base=0,
                               pattern=[[-1, P]], channel_multiplier=1)
            pool.affine_select(out=mask_kq[:], in_=mask_kq[:], compare_op=ALU.is_ge, fill=MASKED, base=0,
                               pattern=[[1, P]], channel_multiplier=-1)
            pool.drain().then_inc(consts, 1)

            def inv_std(dst, src):
                pool.tensor_tensor(vare[:, 0, :], src[:, 1:2], eps_t[:], ALU.add)
                pool.drain()
                return pool.tensor_tensor(dst, vare[:, 0, :], neg_half[:], ALU.pow)

            def head_tile(b, t):
                pool.wait_ge(head_stat, NT * b + t + 1)
                inv_std(rstd[:, t % 2, :], mv[:, t % 2, :]).then_inc(head_rstd, 1)

            def rope_tile(G, t):
                N = NT * G + t
                pool.wait_ge(qkv_evac, N + 1)
                pool.wait_ge(rope_r, wait_value(N - 1))
                pool.tensor_tensor(
                    ropeA[:, t % 2].rearrange("p n (m two) -> p n m two", two=2),
                    qk32[:, t % 3].rearrange("p n (m two) -> p n m two", two=2),
                    cos_sb[:, t:t + 1, :].rearrange("p o (m one) -> p o m one", one=1).to_broadcast(
                        [P, 2 * HG, HS // 2, 2]), ALU.mult).then_inc(rope_a, 1)

            def head_low(b, t):
                pool.wait_ge(head_hi, NT * b + t + 1)
                pool.tensor_tensor(hT[:, 1, :, t * P:(t + 1) * P], x1[:, t % 2, :].rearrange("p (k q) -> p k q", k=KC),
                                   hT[:, 0, :, t * P:(t + 1) * P], ALU.subtract).then_inc(head_done, 1)

            def add_pair(G, j):
                s = PAIRS[j]
                for p in range(2):
                    pool.wait_ge(exp_done, HG * (NS * G + s + 1) + 2 * p + 2)
                    pool.wait_ge(pair_used, wait_value(NP * G + j))
                    pool.tensor_tensor(psum2[:, p], prob[:, s % 3, p], prob[:, (s + 1) % 3, p],
                                       ALU.add).then_inc(pair_sum, 1)

            def out_norm(G, cq):
                pool.wait_ge(recip_done, TPC * (NC_ * G + cq + 1))
                pool.tensor_tensor(osum[:], osum[:], dsum[:], ALU.mult).then_inc(out_normed, 1)

            def out_low(G, cq):
                pool.wait_ge(out_hi, NC_ * G + cq + 1)
                pool.tensor_tensor(ot16[:, 1, :], osum[:], ot16[:, 0, :],
                                   ALU.subtract).then_inc(out_split, 1)

            def tail_x(b, t, job):
                if t == 0:
                    pool.wait_ge(bc_ld, 16 * (b + 1))
                x_, _, _ = tail_buffers(b, t)
                pool.wait_ge(x_ld[t % 2], 16 * (job + 1))
                pool.tensor_tensor(x_, x_, bc[:, 1, :], ALU.add).then_inc(tail_x_bias, 1)

            def tail_stage(b, t, stage, use, job):
                Z = NT * b + t
                i = t % 2
                if stage == 0:
                    tail_x(b, t, job)
                    pool.drain()
                    pool.wait_ge(ring_free, use + 1)
                    pool.wait_ge(out_dma[i], 16 * (NT // 2 * b + t // 2))
                    pool.tensor_tensor(x1[:, i, :], wk[:, i, :], xs[:, i, :], ALU.add).then_inc(tail_x1_sum, 1)
                elif stage == 1:
                    tail_inverse1(b, t)
                elif stage == 3:
                    tail_inverse2(b, t)
                pool.drain()

            def tail_inverse1(b, t):
                pool.wait_ge(tail_stats1, NT * b + t + 1)
                inv_std(rstd[:, t % 2, :], mv[:, t % 2, :]).then_inc(tail_rstd1, 1)
                x_, _, x1_ = tail_buffers(b, t)
                pool.tensor_tensor(x_, x1_, bc[:, 5, :], ALU.add).then_inc(tail_x1_shift, 1)

            def tail_inverse2(b, t):
                pool.drain()
                pool.wait_ge(tail_stats2, NT * b + t + 1)
                inv_std(rstd2[:, t % 2, :], mv2[:, t % 2, :]).then_inc(tail_rstd2, 1)

            for t in range(NT + 1):
                if t < NT:
                    pool.drain()
                    head_tile(0, t)
                if t >= 1:
                    head_low(0, t - 1)
            pool.wait_ge(rope_ld, 32)
            for t in range(NT):
                rope_tile(0, t)
            for par in range(2):
                pool.drain()
                pool.memset(qk[R:RM, par, 1, :, :], M_SCALE)
            pool.drain().then_inc(scale_rows, 1)

            def body(b, first, last):
                jobs = job_base(b)
                n = 0
                bank0 = ring_first(b)
                for g in range(NG):
                    G = NG * b + g
                    nxt = not (last and g == NG - 1)
                    if nxt:
                        for t in range(NT):
                            rope_tile(G + 1, t)
                    pool.drain()
                    tail, head, own = tail_at(g, first, last), head_at(g, last), own_at(g, last)
                    plan = unit_plan(tail, head)
                    uses = {}
                    for s in range(NS):
                        if nxt:
                            n += len(plan[s])
                        if s in tail:
                            uses[tail[s]] = ring_base(b) + n
                        n += (s in tail) + (s in head) + (s in own)
                        if s - 1 in PAIRS and nxt:
                            add_pair(G, PAIRS.index(s - 1))
                        for stage in (0, 1, 3):
                            if s - 2 * stage in tail:
                                t = tail[s - 2 * stage]
                                job = jobs + t // 2 + (NT // 2 if t >= 2 * T0 and not last else 0)
                                tail_stage(b - 1, t, stage, uses[t], job)
                        if s in own:
                            tail_x(b, own[s], jobs + NT // 2 + own[s] // 2)
                        if s - 1 in own:
                            tail_inverse1(b, own[s - 1])
                        if s - 2 in own:
                            tail_inverse2(b, own[s - 2])
                            pool.drain()
                        if s + 2 in head:
                            head_tile(b + 1, head[s + 2])
                            pool.drain()
                        if s - 1 in head:
                            head_low(b + 1, head[s - 1])
                        for stage, out_stage in (("norm", out_norm), ("low", out_low)):
                            cq = leaving(s, stage, bool(own))
                            if cq is not None and not (cq == NC_ - 1 and g == 0 and first):
                                out_stage(G - (cq == NC_ - 1), cq)

            batches(pool, body)
            for t in range(NT - TPC, NT):
                tail_x(B - 1, t, NT * (2 * B - 1) // 2 + (NT - 2 + t % 2) // 2)
            for t in range(NT - TPC, NT + 1):
                pool.drain()
                if t < NT:
                    tail_inverse1(B - 1, t)
                if t > NT - TPC:
                    tail_inverse2(B - 1, t - 1)

        @block.scalar
        def _(act):
            act.wait_ge(c_ld, 16 * KC)
            act.activation(eT[:], cT[:], ACT.Exp, scale=-1.0).then_inc(silu_e, 1)
            act.wait_ge(w_ld, 32)
            act.activation(stage_w16[:, 0], stage_wqkv, ACT.Copy, scale=W_SCALE).then_inc(w_hi, 1)
            act.activation(wp16[:, 0], stage_wproj, ACT.Copy, scale=W_SCALE).then_inc(w_hi, 1)
            act.wait_ge(col_ld, 32)
            act.wait_ge(wproj_split, 1)
            for t in range(NT):
                act.wait_ge(turn_done, t + 1)
                if t >= 2:
                    act.wait_ge(head_done, t - 1)
                for k in range(KC):
                    scaled = act.activation(x1[:, t % 2, k * P:(k + 1) * P], ring[t % NBK][:, k * P:(k + 1) * P],
                                            ACT.Identity, bias=colmod[:, 0, k:k + 1], scale=colmod[:, 1, k:k + 1])
                scaled.then_inc(turn_free, 1)
                act.drain()
                act.copy(hT[:, 0, :, t * P:(t + 1) * P],
                         x1[:, t % 2, :].rearrange("p (k q) -> p k q", k=KC)).then_inc(head_hi, 1)

            def second_hi(G, t):
                N = NT * G + t
                act.wait_ge(rope_r, N + 1)
                act.wait_ge(qk_tr, wait_value(N - 2))
                act.copy(qk16[:, t % 3, :, HS:2 * HS], ropeR[:, t % 3, :, 0, :])
                act.copy(qk16[:, t % 3, :, R + 2 * HS:R + 3 * HS], ropeR[:, t % 3, :, 1, :]).then_inc(hi2_done, 1)

            def transposed(G, par, t):
                act.wait_ge(qk_tr, NT * G + t + 1)
                act.copy(qk[0:R, par, :, :, t * P:(t + 1) * P].rearrange("p two h q -> p (two h) q"),
                         ps_tr[t % 2][0:R, :].rearrange("p (n q) -> p n q", q=P)).then_inc(tr_evac, 1)

            def qkv(G, par):
                for t in range(NT):
                    if t < NT:
                        second_hi(G, t)
                    if t >= 3:
                        transposed(G, par, t - 3)

            def maxima(G):
                act.wait_ge(max_turned, G + 1)
                act.wait_ge(max_dma, 32 * G)
                act.copy(mrow[:], ring[0][:, 0:P // 2].bitcast(F16)).then_inc(max_rows, 1)

            qkv(0, 0)
            for t in range(NT - 3, NT):
                transposed(0, 0, t)

            def body(b, first, last):
                for g in range(NG):
                    G = NG * b + g
                    maxima(G)
                    nxt = not (last and g == NG - 1)
                    if nxt:
                        qkv(G + 1, (g + 1) % 2)
                    for s, (cq, kt) in enumerate(STEPS):
                        w = QC - P * max(kt - TPC * cq, 0)
                        S = NS * G + s
                        for h in range(HG):
                            p = h // 2
                            act.wait_ge(scores_done, HG * S + h + 1)
                            act.wait_ge(prob_used, wait_value(S - 2 if s >= 3 else NS * G))
                            if s < 3:
                                act.wait_ge(pair_sum, wait_value(2 * NP * G))
                            elif nxt and (s - 3 in PAIRS or s - 4 in PAIRS):
                                j = PAIRS.index(s - 3 if s - 3 in PAIRS else s - 4)
                                act.wait_ge(pair_sum, 2 * (NP * G + j) + p + 1)
                            act.activation(prob[:, s % 3, p, h % 2, 0:w], ps_scores[(HG * s + h) % NBK][:, 0:w], ACT.Exp,
                                           scale=SCALE).then_inc(exp_done, 1)
                            if (s, h) in LATE_TURNS and not (last and g == NG - 1):
                                transposed(G + 1, (g + 1) % 2, LATE_TURNS[s, h])
                        if s - 1 in head_at(g, last):
                            head_high(b + 1, head_at(g, last)[s - 1])
                        own = own_at(g, last)
                        out = leaving(s, "leave", bool(own))
                        if out is not None:
                            leave(G, out)
                        out = leaving(s, "high", bool(own))
                        if out is not None and not (out == NC_ - 1 and g == 0 and first):
                            out_high(G - (out == NC_ - 1), out)
                    leave(G, NC_ - 1)

            def head_high(b, t):
                act.wait_ge(head_scaled, NT * (b - 1) + t + 1)
                act.copy(hT[:, 0, :, t * P:(t + 1) * P],
                         x1[:, t % 2, :].rearrange("p (k q) -> p k q", k=KC)).then_inc(head_hi, 1)

            def leave(G, cq):
                last_step = NS * G + max(i for i, (q, _) in enumerate(STEPS) if q == cq)
                act.wait_ge(prob_used, last_step + 1)
                act.wait_ge(out_split, wait_value(NC_ * G + cq))
                act.copy(dsum[:], ps_den[:])
                act.copy(osum[:], ps_out[:]).then_inc(sums_left, 1)

            def out_high(G, cq):
                act.wait_ge(out_normed, NC_ * G + cq + 1)
                act.wait_ge(ot_dma, wait_value(16 * (NC_ * G + cq)))
                act.copy(ot16[:, 0, :], osum[:]).then_inc(out_hi, 1)

            batches(act, body)

        @block.vector
        def _(dve):
            def head_stats(b, t, job):
                dve.wait_ge(x_ld[t % 2], 16 * (job + 1))
                dve.wait_ge(head_rstd, wait_value(NT * b + t - 1))
                dve.bn_stats(stats[:, t % 2, :], xs[:, t % 2, :])
                dve.drain()
                dve.bn_aggr(mv[:, t % 2, :], stats[:, t % 2, :]).then_inc(head_stat, 1)

            def head_normed(b, t):
                dve.wait_ge(head_rstd, NT * b + t + 1)
                dve.tensor_scalar(wk[:, t % 2, :], xs[:, t % 2, :], mv[:, t % 2, 0:1], rstd[:, t % 2, :],
                                  ALU.subtract, ALU.mult).then_inc(head_norm, 1)

            dve.wait_ge(silu_e, 1)
            dve.tensor_scalar(eT[:], eT[:], 1.0, None, ALU.add)
            dve.drain()
            dve.reciprocal(eT[:], eT[:])
            dve.drain()
            dve.tensor_tensor(cT[:], cT[:], eT[:], ALU.mult).then_inc(silu_done, 1)
            dve.wait_ge(w_ld, 32)
            for i, (st, dst, done) in enumerate(((stage_wqkv, stage_w16, wqkv_split), (stage_wproj, wp16, wproj_split))):
                dve.wait_ge(w_hi, i + 1)
                dve.scalar_tensor_tensor(dst[:, 1], st, W_SCALE, dst[:, 0], ALU.mult, ALU.subtract).then_inc(done, 1)
            for t in range(2):
                head_stats(0, t, 0)
                head_normed(0, t)
            dve.wait_ge(row_ld, 48)
            for j in range(6):
                dve.wait_ge(mod_mm, j + 1)
                src = mod_banks[j][0:B, :]
                gate = prow[:, 3, :]
                sign = prow[:, 4, :]
                if j == 0:
                    dve.tensor_copy(rows[:, 0, :], src)
                elif j == 1:
                    dve.tensor_scalar(rows[:, 1, :], src, 1.0, None, ALU.add)
                    dve.drain().then_inc(mod_row, 1)
                elif j == 3:
                    dve.tensor_copy(rows[:, 5, :], src)
                elif j == 4:
                    dve.tensor_scalar(rows[:, 4, :], src, 1.0, None, ALU.add)
                else:
                    dve.tensor_copy(gate, src)
                    dve.drain()
                    dve.tensor_scalar(sign, gate, 0.0, None, ALU.is_ge)
                    dve.tensor_scalar(rows[:, 7, :], gate, 0.0, None, ALU.is_lt)
                    dve.drain()
                    dve.scalar_tensor_tensor(sign, gate, 0.25, sign, ALU.max, ALU.mult)
                    dve.scalar_tensor_tensor(rows[:, 7, :], gate, -0.25, rows[:, 7, :], ALU.min, ALU.mult)
                    dve.drain()
                    dve.tensor_tensor(gate, rows[:, 7, :], sign, ALU.add)
                    dve.drain()
                    if j == 2:
                        dve.tensor_scalar(rows[:, 2, :], gate, 1.0 / W_SCALE, None, ALU.mult)
                        dve.tensor_tensor(rows[:, 3, :], gate, prow[:, 0, :], ALU.mult)
                    else:
                        dve.tensor_tensor(rows[:, 6, :], gate, prow[:, 1, :], ALU.mult)
                        dve.tensor_tensor(rows[:, 7, :], gate, prow[:, 2, :], ALU.mult)
                    dve.drain()
            dve.drain().then_inc(mod_row, 1)
            dve.memset(mpart[:], -3e38)
            dve.drain()

            def head_evac(b, t, use, n):
                if t == 0:
                    dve.wait_ge(col_ld, 32 * (b + 1))
                    for i in range(2):
                        dve.wait_ge(out_dma[i], wait_value(16 * (NT // 2 * (b - 2) + T0)))
                dve.wait_ge(head_done, wait_value(NT * b + t - 1))
                dve.wait_ge(ring_full, use + 1)
                h32 = x1[:, t % 2, :].rearrange("p (k q) -> p k q", k=KC)
                src = ring[n % NBK][:, :].rearrange("p (k q) -> p k q", k=KC)
                for k in range(KC):
                    normed = dve.tensor_scalar(h32[:, k, :], src[:, k, :], colmod[:, 1, k:k + 1], colmod[:, 0, k:k + 1],
                                               ALU.mult, ALU.add)
                normed.then_inc(ring_free, 1)
                dve.drain().then_inc(head_scaled, 1)

            def qkv(G, g, par):
                for t in range(NT + 2):
                    N = NT * G + t
                    if t < NT:
                        dve.wait_ge(qkv_mm, N + 1)
                        dve.wait_ge(hi2_done, wait_value(N if t == 0 else N - 1))
                        src = ps_scores[(t + SHIFT) % NBK][:, 0:GW].rearrange("p (h n) -> p h n", h=HG)
                        bias = bg[:, par, :].rearrange("p (h n) -> p h n", h=HG)
                        dve.scalar_tensor_tensor(qk32[:, t % 3].rearrange("p (h two) n -> p h (two n)", h=HG),
                                                 src[:, :, 0:2 * HS], 1.0 / W_SCALE, bias[:, :, 0:2 * HS],
                                                 ALU.mult, ALU.add)
                        dve.scalar_tensor_tensor(v32[:, par, t, :].rearrange("p (h n) -> p h n", h=HG),
                                                 src[:, :, 2 * HS:3 * HS], 1.0 / W_SCALE, bias[:, :, 2 * HS:3 * HS],
                                                 ALU.mult, ALU.add).then_inc(qkv_evac, 1)
                    if 1 <= t <= NT:
                        dve.wait_ge(rope_a, N)
                        dve.tensor_tensor(ropeR[:, (t - 1) % 3].rearrange("p h two n -> p (h two) n"),
                                          ropeA[:, (t - 1) % 2], ropeB[:], ALU.add).then_inc(rope_r, 1)
                    if t >= 2:
                        u = (t - 2) % 3
                        dve.tensor_tensor(qk16[:, u, :, 2 * HS:3 * HS], ropeR[:, u, :, 0, :], qk16[:, u, :, 0:HS],
                                          ALU.subtract)
                        dve.tensor_tensor(qk16[:, u, :, R + HS:R + 2 * HS], ropeR[:, u, :, 1, :],
                                          qk16[:, u, :, R:R + HS], ALU.subtract).then_inc(lo_done, 1)
                    dve.drain()
                    if t < NT:
                        swapped = qk32[:, t % 3].rearrange("p n (m two) -> p n m two", two=2)[:, :, :, ::-1]
                        dve.tensor_tensor(ropeB[:].rearrange("p n (m two) -> p n m two", two=2), swapped,
                                          sin_sb[:, t:t + 1, :].rearrange("p o (m two) -> p o m two", two=2).to_broadcast(
                                              [P, 2 * HG, HS // 2, 2]), ALU.mult)
                    if 1 <= t <= NT:
                        u = (t - 1) % 3
                        dve.wait_ge(qk_tr, wait_value(N - 3))
                        dve.tensor_copy(qk16[:, u, :, :].rearrange("p h (two r) -> p h two r", two=2)[:, :, :, 0:HS],
                                        ropeR[:, u])
                    dve.drain()

            def unit_max(h, u, use, n):
                qt, kc = UNITS[u]
                w = min(QC, P * (qt + 1) - QC * kc)
                dve.wait_ge(ring_full, use + 1)
                dve.tensor_reduce(mpart[:, h, qt, kc:kc + 1], ring[n % NBK][:, 0:w], AX.X, ALU.max).then_inc(ring_free, 1)

            def maxima(G):
                dve.drain()
                dve.wait_ge(max_turned, wait_value(G))
                dve.tensor_reduce(nmax[:], mpart[:].rearrange("p h t k -> p (h t) k"), AX.X, ALU.max, negate=True)
                dve.drain()
                dve.tensor_scalar(nm16[:, 0, :], nmax[:], 1.0 / M_SCALE, None, ALU.mult)
                dve.drain()
                dve.scalar_tensor_tensor(nm16[:, 1, :], nmax[:], 1.0 / M_SCALE, nm16[:, 0, :], ALU.mult,
                                         ALU.subtract).then_inc(max_split, 1)

            def out_reciprocal(G, cq, part):
                dve.wait_ge(sums_left, NC_ * G + cq + 1)
                cols = slice(part * P, (part + 1) * P)
                dve.reciprocal(dsum[:, cols], dsum[:, cols]).then_inc(recip_done, 1)

            def out_parts(G, g, s, parts, first, own):
                for part in parts:
                    cq = leaving(s, part, own)
                    if cq is not None and not (cq == NC_ - 1 and g == 0 and first):
                        out_reciprocal(G - (cq == NC_ - 1), cq, part)

            def tail_product(b, t, use, n):
                dve.wait_ge(ring_full, use + 1)
                if t >= 2:
                    dve.wait_ge(tail_done, NT * b + t - 1)
                dve.tensor_tensor(wk[:, t % 2, :], ring[n % NBK][:, :], bc[:, 0, :], ALU.mult).then_inc(ring_free, 1)

            def tail_stage(b, t, stage):
                Z = NT * b + t
                i = t % 2
                if stage == 1:
                    dve.wait_ge(tail_x1_sum, Z + 1)
                    dve.bn_stats(stats[:, i, :], x1[:, i, :])
                    dve.drain()
                    dve.bn_aggr(mv[:, i, :], stats[:, i, :]).then_inc(tail_stats1, 1)
                elif stage == 2:
                    dve.wait_ge(tail_rstd1, Z + 1)
                    dve.scalar_tensor_tensor(wk[:, i, :], x1[:, i, :], mv[:, i, 0:1], bc[:, 2, :], ALU.subtract, ALU.mult)
                    dve.drain()
                    dve.scalar_tensor_tensor(wk[:, i, :], wk[:, i, :], rstd[:, i, :], bc[:, 3, :], ALU.mult, ALU.add)
                    dve.drain()
                elif stage == 3:
                    dve.bn_stats(stats[:, i, :], wk[:, i, :])
                    dve.drain()
                    dve.bn_aggr(mv2[:, i, :], stats[:, i, :]).then_inc(tail_stats2, 1)
                else:
                    tail_third(b, t)

            def tail_first(b, t, use, n):
                x_, wk_, x1_ = tail_buffers(b, t)
                Z = NT * b + t
                i = t % 2
                dve.wait_ge(ring_full, use + 1)
                if t < NT - TPC:
                    dve.wait_ge(out_dma[i], 16 * (NT // 2 * b + t // 2))
                dve.wait_ge(tail_x_bias, Z + 1)
                dve.tensor_tensor(wk_, ring[n % NBK][:, :], bc[:, 0, :], ALU.mult).then_inc(ring_free, 1)
                dve.drain()
                dve.tensor_tensor(x1_, wk_, x_, ALU.add)
                dve.drain()
                dve.bn_stats(stats[:, i, :], x1_)
                dve.drain()
                dve.bn_aggr(mv[:, i, :], stats[:, i, :]).then_inc(tail_stats1, 1)

            def tail_second(b, t):
                _, wk_, x1_ = tail_buffers(b, t)
                i = t % 2
                dve.wait_ge(tail_rstd1, NT * b + t + 1)
                dve.scalar_tensor_tensor(wk_, x1_, mv[:, i, 0:1], bc[:, 2, :], ALU.subtract, ALU.mult)
                dve.drain()
                dve.scalar_tensor_tensor(wk_, wk_, rstd[:, i, :], bc[:, 3, :], ALU.mult, ALU.add)
                dve.drain()
                dve.bn_stats(stats[:, i, :], wk_)
                dve.drain()
                dve.bn_aggr(mv2[:, i, :], stats[:, i, :]).then_inc(tail_stats2, 1)

            def tail_third(b, t):
                x_, wk_, x1_ = tail_buffers(b, t)
                i = t % 2
                dve.wait_ge(tail_rstd2, NT * b + t + 1)
                dve.wait_ge(tail_x1_shift, NT * b + t + 1)
                dve.scalar_tensor_tensor(wk_, wk_, mv2[:, i, 0:1], bc[:, 4, :], ALU.subtract, ALU.mult)
                dve.drain()
                dve.scalar_tensor_tensor(x1_, wk_, rstd2[:, i, :], x_, ALU.mult, ALU.add).then_inc(tail_done, 1)

            for t in range(2, NT):
                head_stats(0, t, t // 2)
                dve.wait_ge(turn_done, t - 1)
                head_normed(0, t)
            dve.wait_ge(rope_ld, 32)
            qkv(0, 0, 0)
            for u in range(NS):
                for h in range(HG):
                    unit_max(h, u, HG * u + h, HG * u + h)
            maxima(0)

            def body(b, first, last):
                jobs = job_base(b)
                base = ring_base(b)
                n = 0
                bank0 = ring_first(b)
                for g in range(NG):
                    G = NG * b + g
                    nxt = not (last and g == NG - 1)
                    if nxt:
                        qkv(G + 1, (g + 1) % NG, (g + 1) % 2)
                    tail, head, own = tail_at(g, first, last), head_at(g, last), own_at(g, last)
                    plan = unit_plan(tail, head)
                    for s in range(NS):
                        units = plan[s] if nxt else []
                        for u, h in units[:2]:
                            unit_max(h, u, base + n, bank0 + n)
                            n += 1
                        for stage in range(1, 5):
                            if s - 2 * stage in tail:
                                tail_stage(b - 1, tail[s - 2 * stage], stage)
                        if s + 1 in head:
                            head_normed(b + 1, head[s + 1])
                        out_parts(G, g, s, (0, 2), first, bool(own))
                        for u, h in units[2:3]:
                            unit_max(h, u, base + n, bank0 + n)
                            n += 1
                        if s + 2 in head:
                            first_job = jobs if first else jobs + T0
                            head_stats(b + 1, head[s + 2], first_job + head[s + 2] // 2)
                        out_parts(G, g, s, (1, 3), first, bool(own))
                        for u, h in units[3:]:
                            unit_max(h, u, base + n, bank0 + n)
                            n += 1
                        if s in tail:
                            tail_product(b - 1, tail[s], base + n, bank0 + n)
                            n += 1
                        if s in own:
                            tail_first(b, own[s], base + n, bank0 + n)
                            n += 1
                        if s - 1 in own:
                            tail_second(b, own[s - 1])
                        if s - 2 in own:
                            tail_third(b, own[s - 2])
                        if s in head:
                            head_evac(b + 1, head[s], base + n, bank0 + n)
                            n += 1
                    if nxt:
                        maxima(G + 1)
                return n + bank0

            n = batches(dve, body)
            dve.wait_ge(sums_left, NC_ * NG * B)
            dve.wait_ge(ot_dma, 16 * (NC_ * NG * B - 1))
            for part in range(TPC):
                cols = slice(part * P, (part + 1) * P)
                dve.reciprocal(dsum[:, cols], dsum[:, cols])
                dve.drain()
                dve.tensor_tensor(osum[:, cols], osum[:, cols], dsum[:, cols], ALU.mult)
                dve.drain()
                dve.tensor_copy(ot16[:, 0, cols], osum[:, cols])
                dve.drain()
                dve.tensor_tensor(ot16[:, 1, cols], osum[:, cols], ot16[:, 0, cols], ALU.subtract).then_inc(end_split, 1)
            for t in range(NT - TPC, NT + 2):
                if t < NT:
                    tail_first(B - 1, t, ring_base(B - 1) + n - ring_first(B - 1), n)
                    n += 1
                if NT - TPC < t <= NT:
                    tail_second(B - 1, t - 1)
                if t > NT - TPC + 1:
                    tail_third(B - 1, t - 2)

        @block.tensor
        def _(pe):
            pe.wait_ge(silu_done, 1)
            pe.wait_ge(wm_ld, 16)
            pe.wait_ge(consts, 1)
            for j in range(6):
                for k in range(KC):
                    mm = pe.matmul(mod_banks[j][0:B, :], cT[:, k, :], stage_wmod[:, k, j * C:(j + 1) * C],
                                   start=(k == 0), stop=(k == KC - 1))
                mm.then_inc(mod_mm, 1)

            def head_turn(b, t, use, n):
                pe.wait_ge(head_norm, NT * b + t + 1)
                pe.wait_ge(ring_free, wait_value(use - NBK + 1))
                for k in range(KC):
                    mm = pe.transpose(ring[n % NBK][:, k * P:(k + 1) * P], wk[:, t % 2, k * P:(k + 1) * P], ident[:])
                mm.then_inc(ring_full, 1)

            def turn_maxima(G):
                pe.wait_ge(max_split, G + 1)
                pe.transpose(ring[0][:, 0:P // 2].bitcast(F16), nm16[:].rearrange("p a n -> p (a n)"),
                             ident16[:]).then_inc(max_turned, 1)

            def qkv(G, g, before, loads):
                pe.wait_ge(wg_ld[g % 2], loads)
                if before is not None:
                    pe.wait_ge(sums_left, NC_ * (before - 1) + NC_)
                for t in range(NT):
                    qkv_tile(G, g, t)
                    if t == 1 and before is not None:
                        turn_maxima(before)
                    if t >= 3:
                        turn_tile(G, t - 3)

            def qkv_tile(G, g, t):
                pe.wait_ge(qkv_evac, wait_value(NT * G + t - NBK + 1))
                i = 0
                for a, w in ((0, 0), (0, 1), (1, 0)):
                    for k in range(KC):
                        mm = pe.matmul(ps_scores[(t + SHIFT) % NBK][:, 0:GW], hT[:, a, k, t * P:(t + 1) * P],
                                       wg[:, g % 2, w, k, :], start=(i == 0), stop=(i == 3 * KC - 1))
                        i += 1
                mm.then_inc(qkv_mm, 1)

            def turn_tile(G, t):
                N = NT * G + t
                pe.wait_ge(lo_done, N + 1)
                pe.wait_ge(hi2_done, N + 1)
                pe.wait_ge(tr_evac, wait_value(N - 1))
                for two in range(2):
                    for h in range(HG):
                        o = (two * HG + h) * P
                        mm = pe.transpose(ps_tr[t % 2][0:R, o:o + P], qk16[:, t % 3, h, two * R:(two + 1) * R],
                                          ident16[:])
                mm.then_inc(qk_tr, 1)

            def unit_scores(h, u, par, use, n):
                qt, kc = UNITS[u]
                w = min(QC, P * (qt + 1) - QC * kc)
                diag = kc == qt // TPC
                pe.wait_ge(ring_free, wait_value(use - NBK + 1))
                mm = pe.matmul(ring[n % NBK][:, 0:w], qk[0:R, par, 0, h, qt * P:(qt + 1) * P],
                               qk[0:R, par, 1, h, kc * QC:kc * QC + w], start=True, stop=not diag)
                if diag:
                    mm = pe.matmul(ring[n % NBK][:, w - P:w], identb[:], mask_qk[:], start=False, stop=True)
                mm.then_inc(ring_full, 1)

            def proj(b, t, use, n):
                if t == 0:
                    pe.wait_ge(wproj_split, 1)
                pe.wait_ge(ot_ld[t // 2 % 2], 16 * (NT // 4 * b + t // 4 + 1))
                pe.wait_ge(ring_free, use - NBK + 1)
                q = t % 2 * P
                i = 0
                for a, w in ((0, 0), (0, 1), (1, 0)):
                    for k in range(NG):
                        if k == NG - 1 and isinstance(b, int) and b == B - 1 and t >= NT - TPC:
                            pe.wait_ge(end_split, t - (NT - TPC) + 1)
                            qe = (t - (NT - TPC)) * P
                            att = ot16[:, a, qe:qe + P]
                        else:
                            att = otin[:, t // 2 % 2, k, a, q:q + P]
                        mm = pe.matmul(ring[n % NBK][:, :], att, wp16[:, w, k, :],
                                       start=(i == 0), stop=(i == 3 * NG - 1))
                        i += 1
                mm.then_inc(ring_full, 1)

            def scores(G, par, s, h):
                cq, kt = STEPS[s]
                q0 = P * max(kt - TPC * cq, 0)
                w = QC - q0
                diag = kt >= TPC * cq
                k = HG * s + h
                pe.wait_ge(exp_done, wait_value(HG * NS * G + (k - NBK + 1 if k >= NBK else 0)))
                mm = pe.matmul(ps_scores[k % NBK][:, 0:w], qk[0:RM, par, 1, h, kt * P:(kt + 1) * P],
                               qk[0:RM, par, 0, h, cq * QC + q0:(cq + 1) * QC], start=True, stop=not diag)
                if diag:
                    mm = pe.matmul(ps_scores[k % NBK][:, 0:P], identb[:], mask_kq[:], start=False, stop=True)
                mm.then_inc(scores_done, 1)

            def values(G, par, s, paired):
                cq, kt = STEPS[s]
                q0 = P * max(kt - TPC * cq, 0)
                if kt == 0:
                    pe.wait_ge(sums_left, wait_value(NC_ * G + cq))
                pe.wait_ge(exp_done, HG * (NS * G + s + 1))
                for h in range(HG):
                    mm = pe.matmul(ps_out[h * HS:(h + 1) * HS, q0:QC], v32[:, par, kt, h * HS:(h + 1) * HS],
                                   prob[:, s % 3, h // 2, h % 2, 0:QC - q0], start=kt == 0,
                                   stop=kt == TPC * (cq + 1) - 1)
                if kt < TPC * cq and paired:
                    mm.then_inc(prob_used, 1)

            def denominators(G, s, paired):
                cq, kt = STEPS[s]
                if s - 2 in PAIRS and paired:
                    j = PAIRS.index(s - 2)
                    for h in range(HG):
                        if h % 2 == 0:
                            pe.wait_ge(pair_sum, 2 * (NP * G + j) + h // 2 + 1)
                        mm = pe.matmul(ps_den[h * HS:(h + 1) * HS, :], ones[:], psum2[:, h // 2, h % 2, :],
                                       start=kt == 2, stop=False)
                    mm.then_inc(pair_used, 1)
                if kt >= TPC * cq or not paired:
                    q0 = P * max(kt - TPC * cq, 0)
                    for h in range(HG):
                        mm = pe.matmul(ps_den[h * HS:(h + 1) * HS, q0:QC], ones[:],
                                       prob[:, s % 3, h // 2, h % 2, 0:QC - q0], start=kt == 0,
                                       stop=kt == TPC * (cq + 1) - 1)
                    mm.then_inc(prob_used, 1)

            for t in range(NT):
                pe.wait_ge(head_norm, t + 1)
                if t >= NBK:
                    pe.wait_ge(turn_free, t - NBK + 1)
                for k in range(KC):
                    mm = pe.transpose(ring[t % NBK][:, k * P:(k + 1) * P], wk[:, t % 2, k * P:(k + 1) * P], ident[:])
                mm.then_inc(turn_done, 1)
            pe.wait_ge(head_done, NT)
            qkv(0, 0, None, 32)
            for t in range(NT - 3, NT):
                turn_tile(0, t)
            pe.wait_ge(tr_evac, NT)
            for u in range(NS):
                for h in range(HG):
                    unit_scores(h, u, 0, HG * u + h, HG * u + h)

            def body(b, first, last):
                base = ring_base(b)
                n = 0
                bank0 = ring_first(b)
                for g in range(NG):
                    G = NG * b + g
                    par = g % 2
                    nxt = not (last and g == NG - 1)
                    if nxt:
                        if g == NG - 1:
                            pe.wait_ge(head_done, NT * (b + 2))
                        qkv(G + 1, (g + 1) % NG, G, 32 * (NG // 2 * b + (g + 1) // 2 + 1))
                        first_evac = NT * (G + 2) - NBK
                    else:
                        turn_maxima(G)
                        first_evac = None
                    pe.wait_ge(max_rows, G + 1)
                    pe.wait_ge(max_dma, 32 * (G + 1))
                    if g == 0:
                        pe.wait_ge(scale_rows, 1)
                    tail, head, own = tail_at(g, first, last), head_at(g, last), own_at(g, last)
                    plan = unit_plan(tail, head)
                    for s in range(NS + 1):
                        units = plan[s] if s < NS and nxt else []
                        late = s == 1 and nxt
                        for place in range(5):
                            if place < 4 and s < NS:
                                if s == 0 and place < NBK and first_evac is not None:
                                    pe.wait_ge(qkv_evac, first_evac + place + 1)
                                scores(G, par, s, place)
                            if (s, place) in LATE_TURNS and nxt:
                                turn_tile(G + 1, LATE_TURNS[s, place])
                            if place == 4 and late:
                                pe.wait_ge(tr_evac, NT * (G + 2))
                            if place == (4 if late else 3 if s > 1 and STEPS[s - 1][1] == 0 else 2) and s > 0:
                                values(G, par, s - 1, nxt)
                            if place == (4 if late else 3) and s > 0:
                                denominators(G, s - 1, nxt)
                            if place < len(units):
                                u, h = units[place]
                                unit_scores(h, u, 1 - par, base + n, bank0 + n)
                                n += 1
                        if s in tail or s in own:
                            proj(b if s in own else b - 1, own[s] if s in own else tail[s], base + n, bank0 + n)
                            n += 1
                        if s in head:
                            head_turn(b + 1, head[s], base + n, bank0 + n)
                            n += 1
                return n + bank0

            n = batches(pe, body)
            for t in range(NT - TPC, NT):
                proj(B - 1, t, ring_base(B - 1) + n - ring_first(B - 1), n)
                n += 1


_INS = ["L0_attn_x", "L0_attn_W_qkv", "L0_attn_b_qkv", "L0_attn_W_proj", "L0_attn_b_proj", "L0_ffn_ln_g",
        "L0_ffn_ln_b", "L0_c", "L0_wmod"]


def rope_tables(T, HS):
    import numpy as np
    pos = np.arange(T, dtype=np.float32)[:, None]
    i = np.arange(1, HS // 2 + 1, dtype=np.float32)[None]
    theta = np.float32(1.0) / np.float32(10000.0) ** (np.float32(2.0) * (i - np.float32(1.0)) / np.float32(HS))
    ang = pos * theta
    cos = np.cos(ang)
    sin = np.repeat(np.sin(ang), 2, axis=1)
    sin[:, 0::2] *= -1
    return cos.astype(np.float32), sin.astype(np.float32)


def kernel(**inputs):
    import numpy as _np
    import concourse.bacc as _bacc
    from concourse import mybir as _mybir
    from concourse.bass_utils import run_bass_kernel_spmd as _run

    nc = _bacc.Bacc("TRN2", target_bir_lowering=False, num_devices=1, dynamic_dma_scratch_size=1024)
    arrays, args = {}, []
    tables = rope_tables(inputs["L0_attn_x"].shape[1], 32)
    named = [(name, inputs[name]) for name in _INS] + [("rope_cos", tables[0]), ("rope_sin", tables[1])]
    for name, value in named:
        a = _np.ascontiguousarray(value)
        arrays[f"in_{name}_dram"] = a
        args.append(nc.dram_tensor(f"in_{name}_dram", a.shape, _mybir.dt.from_np(a.dtype), kind="ExternalInput").ap())
    out = nc.dram_tensor("out_0_dram", inputs["L0_attn_x"].shape, _mybir.dt.float32, kind="ExternalOutput").ap()
    adaln_block_kernel(nc, *args, out)
    r = _run(nc, [arrays], core_ids=[0])
    return r.results[0]["out_0_dram"]
```
